# Optimizing a Trainium2 kernel written in Bass

```python
import numpy as np
import jax
import jax.numpy as jnp

def _softmax(x, axis=-1):
    return jax.nn.softmax(x, axis=axis)

def _gelu(x):
    return jax.nn.gelu(x, approximate=True)

def _silu(x):
    return jax.nn.silu(x)

def _sigmoid(x):
    return jax.nn.sigmoid(x)

def _layernorm(x, axis=-1, eps=1e-05):
    m = jnp.mean(x, axis=axis, keepdims=True)
    v = jnp.var(x, axis=axis, keepdims=True)
    return (x - m) / jnp.sqrt(v + eps)

def _scatter_add(tgt, idx, src, axis=0):
    return tgt.at[idx].add(src)

def _segment_sum(src, seg, n):
    return jax.ops.segment_sum(src, seg, n)
kernel_name = 'mk_xattn_ffn_d2_seqx_r8_031943'

def setup_inputs(seed: int=0):
    np.random.seed(seed)
    _w = jnp.asarray

    def _rec_inputs():
        import jax
        import jax.numpy as jnp
        _rk = jax.random.key(seed)
        x = -0.0003929 + 0.9999 * jax.random.normal(jax.random.fold_in(_rk, 1), (32, 64, 128), jnp.float32)
        _lenS = 64 - jax.random.randint(jax.random.fold_in(_rk, 7), (32,), 0, max(1, 64 // 4) + 1, jnp.int32)
        _lenS2 = 64 - jax.random.randint(jax.random.fold_in(_rk, 8), (32,), 0, max(1, 64 // 4) + 1, jnp.int32)
        _ctx_768P = jax.random.normal(jax.random.fold_in(_rk, 11), (32, 16, 96), jnp.float32)
        _ctx_768c = jax.random.dirichlet(jax.random.fold_in(_rk, 511), 0.3 * jnp.ones((16,), jnp.float32), (32, 64))
        _ctx_768t = jnp.einsum('bsk,bkd->bsd', _ctx_768c, _ctx_768P)
        _ctx_768t = _ctx_768t * jax.lax.rsqrt(jnp.mean(jnp.square(_ctx_768t)) + 1e-12) * 0.953939
        ctx_768 = 2.09791e-05 + 1.00001 * (_ctx_768t + 0.3 * jax.random.normal(jax.random.fold_in(_rk, 611), (32, 64, 96), jnp.float32))
        return (x, ctx_768)
    x, ctx_768 = _rec_inputs()

    def _L0_xattn_setup():
        import jax, jax.numpy as jnp
        import numpy as np
        HEADS = 16
        DIM_HEAD = 64
        SCALE = DIM_HEAD ** (-0.5)
        key = jax.random.key(seed)
        ks = jax.random.split(key, 7)
        B, SQ, SKV, QD, CD, ID = (4, 512, 128, 128, 96, HEADS * DIM_HEAD)
        s = lambda d: 1.0 / np.sqrt(d)
        return {'x': jax.random.normal(ks[0], (B, SQ, QD), jnp.float32), 'context': jax.random.normal(ks[1], (B, SKV, CD), jnp.float32), 'Wq': jax.random.normal(ks[2], (QD, ID), jnp.float32) * s(QD), 'Wk': jax.random.normal(ks[3], (CD, ID), jnp.float32) * s(CD), 'Wv': jax.random.normal(ks[4], (CD, ID), jnp.float32) * s(CD), 'Wo': jax.random.normal(ks[5], (ID, QD), jnp.float32) * s(ID), 'bo': jnp.zeros((QD,), jnp.float32)}
    _L0_xattn_all = _L0_xattn_setup()
    _L0_xattn_in = {k: v for k, v in _L0_xattn_all.items() if k in ('Wq', 'Wk', 'Wv', 'Wo', 'bo')}
    del _L0_xattn_all

    def _L0_ffn_setup():
        import jax, jax.numpy as jnp
        import numpy as np
        B, S, D, H, E = (8, 256, 128, 512, 16)
        key = jax.random.key(seed)
        ks = jax.random.split(key, 4)
        sd = 1.0 / np.sqrt(D).astype(np.float32)
        sh = 1.0 / np.sqrt(H).astype(np.float32)
        return {'x': jax.random.normal(ks[0], (B, S, D), jnp.float32), 'Wg': jax.random.normal(ks[1], (D, E), jnp.float32) * sd, 'bg': jnp.zeros((E,), jnp.float32), 'W1': jax.random.normal(ks[2], (E, D, H), jnp.float32) * sd, 'b1': jnp.zeros((E, H), jnp.float32), 'W2': jax.random.normal(ks[3], (E, H, D), jnp.float32) * sh, 'b2': jnp.zeros((E, D), jnp.float32)}
    _L0_ffn_all = _L0_ffn_setup()
    _L0_ffn_in = {k: v for k, v in _L0_ffn_all.items() if k in ('Wg', 'bg', 'W1', 'b1', 'W2', 'b2')}
    del _L0_ffn_all

    def _L1_xattn_setup():
        import jax, jax.numpy as jnp
        import numpy as np
        DIM_Q = 128
        DIM_KV = 96
        N_HEADS = 4

        def _split_heads(x):
            b, l, d = x.shape
            return x.reshape(b, l, N_HEADS, d // N_HEADS).transpose(0, 2, 1, 3)
        key = jax.random.key(seed)
        ks = jax.random.split(key, 7)
        b, lq, lkv = (4, 256, 256)
        q = jax.random.normal(ks[0], (b, lq, DIM_Q), dtype=jnp.float32)
        kv = jax.random.normal(ks[1], (b, lkv, DIM_KV), dtype=jnp.float32)
        s_q = 1.0 / np.sqrt(DIM_Q)
        s_kv = 1.0 / np.sqrt(DIM_KV)
        Wq = jax.random.normal(ks[2], (DIM_Q, DIM_Q), dtype=jnp.float32) * s_q
        Wk = jax.random.normal(ks[3], (DIM_Q, DIM_KV), dtype=jnp.float32) * s_kv
        Wv = jax.random.normal(ks[4], (DIM_Q, DIM_KV), dtype=jnp.float32) * s_kv
        Wo = jax.random.normal(ks[5], (DIM_Q, DIM_Q), dtype=jnp.float32) * s_q
        bo = jax.random.normal(ks[6], (DIM_Q,), dtype=jnp.float32) * 0.01
        return {'q': q, 'kv': kv, 'Wq': Wq, 'Wk': Wk, 'Wv': Wv, 'Wo': Wo, 'bo': bo}
    _L1_xattn_all = _L1_xattn_setup()
    _L1_xattn_in = {k: v for k, v in _L1_xattn_all.items() if k in ('Wq', 'Wk', 'Wv', 'Wo', 'bo')}
    del _L1_xattn_all

    def _L1_ffn_setup():
        import jax, jax.numpy as jnp
        import numpy as np
        DIM = 128
        DEPTH = 6
        HEADS = 16
        DIM_HEAD = 64
        WINDOW = 32
        INNER = HEADS * DIM_HEAD
        DIM_INNER = int(DIM * 4 * 2 / 3)
        QK_SCALE = 8.0

        def shift_tokens(t):
            a, s = jnp.split(t, 2, -1)
            s = jnp.pad(s, ((0, 0), (1, 0), (0, 0)))[:, :-1]
            return jnp.concatenate([a, s], -1)

        def l2norm(t):
            return t / jnp.maximum(jnp.linalg.norm(t, axis=-1, keepdims=True), 1e-12)

        def rotate_half(x):
            x1, x2 = jnp.split(x, 2, -1)
            return jnp.concatenate([-x2, x1], -1)

        def rotary_tables(n):
            half = jnp.arange(0, DIM_HEAD, 2, dtype=jnp.float32)
            inv_freq = 1.0 / 10000.0 ** (half / DIM_HEAD)
            t = jnp.arange(n, dtype=jnp.float32)
            freqs = t[:, None] * inv_freq[None, :]
            freqs = jnp.concatenate([freqs, freqs], -1)
            base_scale = (half + 0.4 * DIM_HEAD) / (1.4 * DIM_HEAD)
            power = (t - n // 2) / (WINDOW // 2)
            scale = base_scale[None, :] ** power[:, None]
            scale = jnp.concatenate([scale, scale], -1)
            return (freqs, scale)

        def local_attention(q, k, v):
            b, h, n, d = q.shape
            w = WINDOW
            nw = n // w
            bq = q.reshape(b, h, nw, w, d)
            bk = k.reshape(b, h, nw, w, d)
            bv = v.reshape(b, h, nw, w, d)

            def look(t):
                p = jnp.pad(t, ((0, 0), (0, 0), (1, 0), (0, 0), (0, 0)))
                return jnp.concatenate([p[:, :, :nw], p[:, :, 1:]], axis=3)
            bk2, bv2 = (look(bk), look(bv))
            seq = jnp.arange(n).reshape(nw, w)
            seq_p = jnp.pad(seq, ((1, 0), (0, 0)), constant_values=-1)
            jt = jnp.concatenate([seq_p[:nw], seq_p[1:]], axis=1)
            it = seq[:, :, None]
            jb = jt[:, None, :]
            mask = (it < jb) | (it > jb + w) | (jb == -1)
            sim = jnp.einsum('bhwie,bhwje->bhwij', bq, bk2) * QK_SCALE
            sim = jnp.where(mask, -jnp.finfo(sim.dtype).max, sim)
            attn = jax.nn.softmax(sim, -1)
            out = jnp.einsum('bhwij,bhwje->bhwie', attn, bv2)
            return out.reshape(b, h, n, d)

        def attn_layer(x, Wqkv, qs, ksc, Wo):
            b, n, _ = x.shape
            qkv = x @ Wqkv
            q, k, v = jnp.split(qkv, 3, -1)
            sh = lambda t: t.reshape(b, n, HEADS, DIM_HEAD).transpose(0, 2, 1, 3)
            q, k, v = (sh(q), sh(k), sh(v))
            q = l2norm(q) * qs
            k = l2norm(k) * ksc
            freqs, scale = rotary_tables(n)
            cos, sin = (jnp.cos(freqs), jnp.sin(freqs))
            q = q * cos * scale + rotate_half(q) * sin * scale
            inv = 1.0 / scale
            k = k * cos * inv + rotate_half(k) * sin * inv
            out = local_attention(q, k, v)
            out = out.transpose(0, 2, 1, 3).reshape(b, n, INNER)
            return out @ Wo

        def ffn_layer(x, g, bln, W1, b1, W2, b2):
            mu = x.mean(-1, keepdims=True)
            var = ((x - mu) ** 2).mean(-1, keepdims=True)
            xn = (x - mu) / jnp.sqrt(var + 1e-05) * g + bln
            hg = xn @ W1 + b1
            a, gate = jnp.split(hg, 2, -1)
            return a * jax.nn.gelu(gate, approximate=False) @ W2 + b2
        key = jax.random.key(seed)
        ks = jax.random.split(key, 8)
        B, N = (2, 256)
        init = lambda k, shape: jax.random.normal(k, shape, jnp.float32) * 0.02
        return {'x': jax.random.normal(ks[0], (B, N, DIM), jnp.float32), 'Wqkv': init(ks[1], (DEPTH, DIM, 3 * INNER)), 'q_scale': jnp.ones((DEPTH, DIM_HEAD), jnp.float32), 'k_scale': jnp.ones((DEPTH, DIM_HEAD), jnp.float32), 'Wo': init(ks[2], (DEPTH, INNER, DIM)), 'ln_g': jnp.ones((DEPTH, DIM), jnp.float32), 'ln_b': jnp.zeros((DEPTH, DIM), jnp.float32), 'W1': init(ks[3], (DEPTH, DIM, 2 * DIM_INNER)), 'b1': jnp.zeros((DEPTH, 2 * DIM_INNER), jnp.float32), 'W2': init(ks[4], (DEPTH, DIM_INNER, DIM)), 'b2': jnp.zeros((DEPTH, DIM), jnp.float32)}
    _L1_ffn_all = _L1_ffn_setup()
    _L1_ffn_in = {k: v for k, v in _L1_ffn_all.items() if k in ('Wqkv', 'q_scale', 'k_scale', 'Wo', 'ln_g', 'ln_b', 'W1', 'b1', 'W2', 'b2')}
    del _L1_ffn_all
    return {'x': x, 'ctx_768': ctx_768, 'L0_xattn_Wq': _L0_xattn_in['Wq'], 'L0_xattn_Wk': _L0_xattn_in['Wk'], 'L0_xattn_Wv': _L0_xattn_in['Wv'], 'L0_xattn_Wo': _L0_xattn_in['Wo'], 'L0_xattn_bo': _L0_xattn_in['bo'], 'L0_ffn_Wg': _L0_ffn_in['Wg'], 'L0_ffn_bg': _L0_ffn_in['bg'], 'L0_ffn_W1': _L0_ffn_in['W1'], 'L0_ffn_b1': _L0_ffn_in['b1'], 'L0_ffn_W2': _L0_ffn_in['W2'], 'L0_ffn_b2': _L0_ffn_in['b2'], 'L1_xattn_Wq': _L1_xattn_in['Wq'], 'L1_xattn_Wk': _L1_xattn_in['Wk'], 'L1_xattn_Wv': _L1_xattn_in['Wv'], 'L1_xattn_Wo': _L1_xattn_in['Wo'], 'L1_xattn_bo': _L1_xattn_in['bo'], 'L1_ffn_Wqkv': _L1_ffn_in['Wqkv'], 'L1_ffn_q_scale': _L1_ffn_in['q_scale'], 'L1_ffn_k_scale': _L1_ffn_in['k_scale'], 'L1_ffn_Wo': _L1_ffn_in['Wo'], 'L1_ffn_ln_g': _L1_ffn_in['ln_g'], 'L1_ffn_ln_b': _L1_ffn_in['ln_b'], 'L1_ffn_W1': _L1_ffn_in['W1'], 'L1_ffn_b1': _L1_ffn_in['b1'], 'L1_ffn_W2': _L1_ffn_in['W2'], 'L1_ffn_b2': _L1_ffn_in['b2']}

def reference(x, ctx_768, L0_xattn_Wq, L0_xattn_Wk, L0_xattn_Wv, L0_xattn_Wo, L0_xattn_bo, L0_ffn_Wg, L0_ffn_bg, L0_ffn_W1, L0_ffn_b1, L0_ffn_W2, L0_ffn_b2, L1_xattn_Wq, L1_xattn_Wk, L1_xattn_Wv, L1_xattn_Wo, L1_xattn_bo, L1_ffn_Wqkv, L1_ffn_q_scale, L1_ffn_k_scale, L1_ffn_Wo, L1_ffn_ln_g, L1_ffn_ln_b, L1_ffn_W1, L1_ffn_b1, L1_ffn_W2, L1_ffn_b2):
    import jax
    import jax.numpy as jnp

    def _L0_xattn_ref(x, context, Wq, Wk, Wv, Wo, bo):
        import jax, jax.numpy as jnp
        import numpy as np
        HEADS = 16
        DIM_HEAD = 64
        SCALE = DIM_HEAD ** (-0.5)
        b, sq, _ = x.shape

        def split_heads(t):
            return t.reshape(b, -1, HEADS, DIM_HEAD).transpose(0, 2, 1, 3)
        q = split_heads(x @ Wq)
        k = split_heads(context @ Wk)
        v = split_heads(context @ Wv)
        sim = jnp.einsum('bhid,bhjd->bhij', q, k) * SCALE
        attn = jax.nn.softmax(sim, axis=-1)
        out = jnp.einsum('bhij,bhjd->bhid', attn, v)
        out = out.transpose(0, 2, 1, 3).reshape(b, sq, HEADS * DIM_HEAD)
        return out @ Wo + bo

    def _L0_ffn_ref(x, Wg, bg, W1, b1, W2, b2):
        import jax, jax.numpy as jnp
        import numpy as np
        B, S, D, H, E = (8, 256, 128, 512, 16)
        d = x.shape[-1]
        xf = x.reshape(-1, d)
        n_tok = xf.shape[0]
        n_exp = Wg.shape[1]
        cap = -(-n_tok // n_exp)
        score = jax.nn.softmax(xf @ Wg + bg, axis=-1)
        gate = jnp.max(score, axis=-1)
        idx = jnp.argmax(score, axis=-1)
        onehot = jax.nn.one_hot(idx, n_exp, dtype=jnp.int32)
        pos = jnp.sum((jnp.cumsum(onehot, axis=0) - 1) * onehot, axis=-1)
        keep = pos < cap
        safe_pos = jnp.where(keep, pos, cap - 1)
        buf = jnp.zeros((n_exp, cap, d), x.dtype).at[idx, safe_pos].add(jnp.where(keep[:, None], xf, 0.0))
        h = jax.nn.relu(jnp.einsum('ecd,edh->ech', buf, W1) + b1[:, None, :])
        y = jnp.einsum('ech,ehd->ecd', h, W2) + b2[:, None, :]
        out = y[idx, safe_pos] * gate[:, None]
        out = jnp.where(keep[:, None], out, 0.0)
        return out.reshape(x.shape)

    def _L1_xattn_ref(q, kv, Wq, Wk, Wv, Wo, bo):
        import jax, jax.numpy as jnp
        import numpy as np
        DIM_Q = 128
        DIM_KV = 96
        N_HEADS = 4

        def _split_heads(x):
            b, l, d = x.shape
            return x.reshape(b, l, N_HEADS, d // N_HEADS).transpose(0, 2, 1, 3)
        qp = q @ Wq.T
        kp = kv @ Wk.T
        vp = kv @ Wv.T
        qh, kh, vh = (_split_heads(qp), _split_heads(kp), _split_heads(vp))
        scale = (DIM_Q // N_HEADS) ** (-0.5)
        scores = jnp.einsum('bhqd,bhkd->bhqk', qh, kh) * scale
        attn = jax.nn.softmax(scores, axis=-1)
        ctx = jnp.einsum('bhqk,bhkd->bhqd', attn, vh)
        b, h, lq, hd = ctx.shape
        ctx = ctx.transpose(0, 2, 1, 3).reshape(b, lq, h * hd)
        return ctx @ Wo.T + bo

    def _L1_ffn_ref(x, Wqkv, q_scale, k_scale, Wo, ln_g, ln_b, W1, b1, W2, b2):
        import jax, jax.numpy as jnp
        import numpy as np
        DIM = 128
        DEPTH = 6
        HEADS = 16
        DIM_HEAD = 64
        WINDOW = 32
        INNER = HEADS * DIM_HEAD
        DIM_INNER = int(DIM * 4 * 2 / 3)
        QK_SCALE = 8.0

        def shift_tokens(t):
            a, s = jnp.split(t, 2, -1)
            s = jnp.pad(s, ((0, 0), (1, 0), (0, 0)))[:, :-1]
            return jnp.concatenate([a, s], -1)

        def l2norm(t):
            return t / jnp.maximum(jnp.linalg.norm(t, axis=-1, keepdims=True), 1e-12)

        def rotate_half(x):
            x1, x2 = jnp.split(x, 2, -1)
            return jnp.concatenate([-x2, x1], -1)

        def rotary_tables(n):
            half = jnp.arange(0, DIM_HEAD, 2, dtype=jnp.float32)
            inv_freq = 1.0 / 10000.0 ** (half / DIM_HEAD)
            t = jnp.arange(n, dtype=jnp.float32)
            freqs = t[:, None] * inv_freq[None, :]
            freqs = jnp.concatenate([freqs, freqs], -1)
            base_scale = (half + 0.4 * DIM_HEAD) / (1.4 * DIM_HEAD)
            power = (t - n // 2) / (WINDOW // 2)
            scale = base_scale[None, :] ** power[:, None]
            scale = jnp.concatenate([scale, scale], -1)
            return (freqs, scale)

        def local_attention(q, k, v):
            b, h, n, d = q.shape
            w = WINDOW
            nw = n // w
            bq = q.reshape(b, h, nw, w, d)
            bk = k.reshape(b, h, nw, w, d)
            bv = v.reshape(b, h, nw, w, d)

            def look(t):
                p = jnp.pad(t, ((0, 0), (0, 0), (1, 0), (0, 0), (0, 0)))
                return jnp.concatenate([p[:, :, :nw], p[:, :, 1:]], axis=3)
            bk2, bv2 = (look(bk), look(bv))
            seq = jnp.arange(n).reshape(nw, w)
            seq_p = jnp.pad(seq, ((1, 0), (0, 0)), constant_values=-1)
            jt = jnp.concatenate([seq_p[:nw], seq_p[1:]], axis=1)
            it = seq[:, :, None]
            jb = jt[:, None, :]
            mask = (it < jb) | (it > jb + w) | (jb == -1)
            sim = jnp.einsum('bhwie,bhwje->bhwij', bq, bk2) * QK_SCALE
            sim = jnp.where(mask, -jnp.finfo(sim.dtype).max, sim)
            attn = jax.nn.softmax(sim, -1)
            out = jnp.einsum('bhwij,bhwje->bhwie', attn, bv2)
            return out.reshape(b, h, n, d)

        def attn_layer(x, Wqkv, qs, ksc, Wo):
            b, n, _ = x.shape
            qkv = x @ Wqkv
            q, k, v = jnp.split(qkv, 3, -1)
            sh = lambda t: t.reshape(b, n, HEADS, DIM_HEAD).transpose(0, 2, 1, 3)
            q, k, v = (sh(q), sh(k), sh(v))
            q = l2norm(q) * qs
            k = l2norm(k) * ksc
            freqs, scale = rotary_tables(n)
            cos, sin = (jnp.cos(freqs), jnp.sin(freqs))
            q = q * cos * scale + rotate_half(q) * sin * scale
            inv = 1.0 / scale
            k = k * cos * inv + rotate_half(k) * sin * inv
            out = local_attention(q, k, v)
            out = out.transpose(0, 2, 1, 3).reshape(b, n, INNER)
            return out @ Wo

        def ffn_layer(x, g, bln, W1, b1, W2, b2):
            mu = x.mean(-1, keepdims=True)
            var = ((x - mu) ** 2).mean(-1, keepdims=True)
            xn = (x - mu) / jnp.sqrt(var + 1e-05) * g + bln
            hg = xn @ W1 + b1
            a, gate = jnp.split(hg, 2, -1)
            return a * jax.nn.gelu(gate, approximate=False) @ W2 + b2
        for i in range(DEPTH):
            x = attn_layer(shift_tokens(x), Wqkv[i], q_scale[i], k_scale[i], Wo[i]) + x
            x = ffn_layer(shift_tokens(x), ln_g[i], ln_b[i], W1[i], b1[i], W2[i], b2[i]) + x
        return x
    x = x + _L0_xattn_ref(_layernorm(x, axis=-1), ctx_768, L0_xattn_Wq, L0_xattn_Wk, L0_xattn_Wv, L0_xattn_Wo, L0_xattn_bo)
    x = x + _L0_ffn_ref(_layernorm(x, axis=-1), L0_ffn_Wg, L0_ffn_bg, L0_ffn_W1, L0_ffn_b1, L0_ffn_W2, L0_ffn_b2)
    x = x + _L1_xattn_ref(_layernorm(x, axis=-1), ctx_768, L1_xattn_Wq, L1_xattn_Wk, L1_xattn_Wv, L1_xattn_Wo, L1_xattn_bo)
    x = x + _L1_ffn_ref(_layernorm(x, axis=-1), L1_ffn_Wqkv, L1_ffn_q_scale, L1_ffn_k_scale, L1_ffn_Wo, L1_ffn_ln_g, L1_ffn_ln_b, L1_ffn_W1, L1_ffn_b1, L1_ffn_W2, L1_ffn_b2)
    return x

_drawn_inputs = setup_inputs


def setup_inputs(seed=0):
    import zlib

    import numpy as np

    out = dict(_drawn_inputs(seed))
    spreads = {'L0_xattn_bo': (0.0, 0.1),
     'L0_ffn_bg': (0.0, 0.1),
     'L0_ffn_b1': (0.0, 0.566),
     'L0_ffn_b2': (0.0, 0.394),
     'L1_ffn_q_scale': (1.0, 0.6),
     'L1_ffn_k_scale': (1.0, 0.6),
     'L1_ffn_ln_g': (1.0, 0.6),
     'L1_ffn_ln_b': (0.0, 0.8),
     'L1_ffn_b1': (0.0, 0.8),
     'L1_ffn_b2': (0.0, 0.1)}
    factors = {'L1_xattn_bo': 6.808, 'L1_ffn_W1': 4.175, 'L1_ffn_W2': 4.121}
    for name, (base, spread) in spreads.items():
        noise = np.random.default_rng([zlib.crc32(name.encode()), seed]).standard_normal(out[name].shape)
        drawn = base * np.exp(spread * noise) if base else spread * noise
        out[name] = jnp.asarray(drawn.astype(out[name].dtype))
    for name, factor in factors.items():
        out[name] = (out[name] * factor).astype(out[name].dtype)
    return out
```

```python
from contextlib import ExitStack

import numpy as np

import concourse.bass as bass
from concourse import mybir

F32 = mybir.dt.float32
BF16 = mybir.dt.bfloat16
I32 = mybir.dt.int32
ALU = mybir.AluOpType
ACT = mybir.ActivationFunctionType
AX_X = mybir.AxisListType.X

P = 128
D = 128
BATCH, SEQ = 32, 64
TILES = BATCH * SEQ // P
CTX_D = 96
HEADS, HEAD_D = 16, 64
INNER = HEADS * HEAD_D
PAIRS = HEADS // 2
XHEADS, XHEAD_D = 4, 32
EXPERTS, HIDDEN = 16, 512
CAP = BATCH * SEQ // EXPERTS
SLOTS = EXPERTS * CAP
DEPTH = 6
WINDOW = 32
FF = D * 4 * 2 // 3
FF_CHUNKS = 3
GROUP = 4
LN_EPS = 1e-5
NORM_FLOOR = 1e-24
LN_SHIFT = 17
MASKED = -1e30

C_IDENT, C_SHIFT, C_TRI, C_ONES, C_MASK = 0, 128, 256, 384, 512
C_ROPE, C_EXPERT, C_END = 1024, 1280, 1296
B_MOE1, B_FF1, B_LNG, B_LNB, B_END = 0, 64, 100, 106, 112
R_BO0, R_BG, R_MOE2, R_BO1, R_FF2, R_END = 0, 128, 144, 2192, 2320, 3088


class Mark:

    def __init__(self, sem, value):
        self.sem, self.value = sem, value


class Queue:

    def __init__(self, counts):
        self.steps, self.waited, self.counts = [], {}, counts

    def wait(self, *marks):
        for m in marks:
            if isinstance(m, (list, tuple)):
                self.wait(*m)
            elif m is not None and self.waited.get(m.sem, 0) < m.value:
                self.waited[m.sem] = m.value
                self.steps.append((None, m.sem, m.value))

    def do(self, instruction, sem=None, by=1):
        self.steps.append((instruction, sem, by))
        if sem is None:
            return None
        self.counts[sem] = self.counts.get(sem, 0) + by
        return Mark(sem, self.counts[sem])

    def play(self, engine, sems):
        for instruction, sem, value in self.steps:
            if instruction is None:
                engine.wait_ge(sems[sem], value)
            elif sem is None:
                instruction(engine)
            else:
                instruction(engine).then_inc(sems[sem], value)


class Ring:

    def __init__(self, buffers):
        self.buffers, self.free, self.turn = buffers, [[] for _ in buffers], -1

    def take(self):
        self.turn = (self.turn + 1) % len(self.buffers)
        return self.turn, self.buffers[self.turn], self.free[self.turn]

    def done(self, n, *marks):
        self.free[n] = list(marks)


def build(nc, t, out):
    counts = {}
    pe, act, dve, pool, sp = (Queue(counts) for _ in range(5))
    ctx = ExitStack()
    with ctx:
        def sb(name, shape, dt=F32):
            return ctx.enter_context(nc.sbuf_tensor(name, shape, dt))

        x = sb("x", [P, TILES, D])
        x_in = sb("x_in", [P, TILES, D])
        ctx_t = sb("ctx_t", [CTX_D, BATCH * SEQ])
        const = sb("const", [P, C_END])
        cols = sb("cols", [P, B_END])
        rows = sb("rows", [1, R_END])
        scales = sb("scales", [P, 2, DEPTH, HEAD_D])
        rope = sb("rope", [P, DEPTH, 4, HEAD_D])
        mask_b = sb("mask_b", [P, 512], BF16)
        ident_b = sb("ident_b", [P, P], BF16)
        tri_b = sb("tri_b", [P, P], BF16)
        ones_b = sb("ones_b", [P, P], BF16)
        w_in = [sb(f"w_in{n}", [P, 3 * INNER]) for n in range(2)]
        w_out = [sb(f"w_out{n}", [P, PAIRS, D]) for n in range(2)]
        w_ff1 = [sb(f"w_ff1{n}", [P, 2 * FF_CHUNKS, P]) for n in range(2)]
        w_ff2 = [sb(f"w_ff2{n}", [P, FF_CHUNKS, D]) for n in range(2)]
        wx = sb("wx", [P, 4, D])
        wg = sb("wg", [D, EXPERTS])

        def ring(name, n, shape, dt=F32):
            return Ring([sb(f"{name}{i}", shape, dt) for i in range(n)])

        r_stat = ring("stat", 4, [P, 12])
        r_xn = ring("xn", 2, [P, D])
        r_xt = ring("xt", 2, [P, P])
        r_sq = ring("sq", 2, [P, INNER])
        r_cos = ring("cos", 4, [P, INNER])
        r_sin = ring("sin", 2, [P, INNER])
        r_norm = ring("norm", 4, [P, 4 * HEADS])
        r_qt = ring("qt", 2, [P, PAIRS, P])
        r_kt = ring("kt", 2, [P, PAIRS, P])
        r_v = ring("v", 3, [P, INNER])
        r_p = ring("p", 2, [P, INNER])
        r_soft = ring("soft", 3, [P, 3 * HEADS])
        r_pt = ring("pt", 1, [P, INNER])
        r_ot = ring("ot", 1, [P, PAIRS, P])
        r_ffx = ring("ffx", 1, [P, GROUP * P])
        r_gate = ring("gate", 2, [P, GROUP * P])
        r_hid = ring("hid", 1, [P, FF_CHUNKS, GROUP * P])
        r_big = Ring([ctx.enter_context(nc.psum_tensor(f"big{i}", [P, 1024], F32)) for i in range(3)])
        r_small = Ring([ctx.enter_context(nc.psum_tensor(f"small{i}", [P, 512], F32)) for i in range(2)])

        ident = const[:, C_IDENT:C_IDENT + P]
        shift = const[:, C_SHIFT:C_SHIFT + P]
        ones_row = const[0:1, C_ONES:C_ONES + P]

        m_const = sp.do(lambda e: e.dma_start(const[:, :], t["const"]), "const_loaded", 16)
        x_loaded = []
        x_d = t["x"].rearrange("(t p) d -> p t d", p=P)
        for q in range(4):
            a, b = 4 * q, 4 * q + 4
            x_loaded += 4 * [sp.do(lambda e, a=a, b=b: e.dma_start(x[:, a:b, :], x_d[:, a:b, :]),
                                   f"x_loaded{q}", 16)]
        for n, name in enumerate(("wq", "wk", "wv")):
            k = D if n == 0 else CTX_D
            m_wa = sp.do(lambda e, n=n, k=k, name=name: e.dma_start(
                w_in[1][0:k, n * INNER:(n + 1) * INNER], t[name]), "first_weights", 16)
        m_wa = sp.do(lambda e: e.dma_start(
            w_out[1][:, :, :], t["wo"].rearrange("(j p) n -> p j n", p=P)), "first_weights", 16)
        m_ctx = sp.do(lambda e: e.dma_start(ctx_t[:, :], t["ctx_t"]), "context_loaded", 16)
        for dst, src in ((cols[:, :], t["cols"]), (rows[:, :], t["rows"]), (wx[:, :, :], t["wx"]),
                         (wg[:, :], t["wg"]), (scales[:, :, :, :], t["scales"].to_broadcast([P, 2, DEPTH, HEAD_D]))):
            m_param = sp.do(lambda e, dst=dst, src=src: e.dma_start(dst, src), "parameters_loaded", 16)

        layer_free = [[], []]
        layer_loaded = {}

        def load_layer(n):
            b = n % 2
            sp.wait(layer_free[b])
            sem = f"layer_weights{b}"
            sp.do(lambda e: e.dma_start(w_in[b][:, :], t["wqkv"][n]), sem, 16)
            sp.do(lambda e: e.dma_start(w_out[b][:, :, :], t["lwo"][n].rearrange("(j p) n -> p j n", p=P)), sem, 16)
            sp.do(lambda e: e.dma_start(w_ff1[b][:, :, :], t["ff1"][n]), sem, 16)
            layer_loaded[n] = sp.do(lambda e: e.dma_start(
                w_ff2[b][:, :, :], t["ff2"][n].rearrange("(c p) n -> p c n", p=P)), sem, 16)

        load_layer(0)

        dve.wait(m_const)
        for dst, at, n in ((mask_b, C_MASK, 512), (ident_b, C_IDENT, P), (tri_b, C_TRI, P), (ones_b, C_ONES, P)):
            m_bf = dve.do(lambda e, dst=dst, at=at, n=n: e.tensor_copy(dst[:, :], const[:, at:at + n]), "bf16_constants")
        pool.wait(m_const, m_param)
        for n in range(DEPTH):
            for s in range(2):
                base = const[:, C_ROPE + 2 * s * HEAD_D:C_ROPE + 2 * (s + 1) * HEAD_D]
                m_rope = pool.do(lambda e, n=n, s=s, base=base: e.tensor_tensor(
                    rope[:, n, 2 * s, :], base[:, 0:HEAD_D], scales[:, s, n, :], ALU.mult), "rope_tables")
                half = HEAD_D // 2
                for h in range(2):
                    m_rope = pool.do(lambda e, n=n, s=s, base=base, h=h: e.tensor_tensor(
                        rope[:, n, 2 * s + 1, h * half:(h + 1) * half],
                        base[:, HEAD_D + h * half:HEAD_D + (h + 1) * half],
                        scales[:, s, n, (1 - h) * half:(2 - h) * half], ALU.mult), "rope_tables")

        x_ready = list(x_loaded)
        x_read = [[] for _ in range(TILES)]

        def inverse_root(src, dst, mark, bias=0.0, scale=1.0, shift_log2=0):
            act.wait(mark)
            m = act.do(lambda e: e.activation(dst, src, ACT.Ln, bias=bias, scale=scale), "log")
            act.wait(m)
            return act.do(lambda e: e.activation(dst, dst, ACT.Exp, bias=0.5 * shift_log2 * float(np.log(2.0)),
                                                 scale=-0.5), "inverse_root")

        def layer_norm(src, mark, place=None):
            sn, st, sfree = r_stat.take()
            dve.wait(mark, sfree)
            m = dve.do(lambda e: e.bn_stats(st[:, 0:6], src), "norm_stats")
            dve.wait(m)
            m = dve.do(lambda e: e.bn_aggr(st[:, 6:8], st[:, 0:6]), "norm_stats")
            m = inverse_root(st[:, 7:8], st[:, 8:9], m, bias=st[:, 9:10])
            n, xn, free = r_xn.take() if place is None else (None, None, None)
            dve.wait(m, free)
            dst = xn[:, :] if place is None else place
            m = dve.do(lambda e: e.tensor_scalar(dst, src, st[:, 6:7], st[:, 8:9], ALU.subtract, ALU.mult),
                       "normalized")
            r_stat.done(sn, m)
            return n, xn, m

        for st in r_stat.buffers:
            m_eps = dve.do(lambda e, st=st: e.memset(st[:, 9:10], LN_EPS), "epsilon")
        act.wait(m_eps)
        floor_shift = sb("floor_shift", [P, 1])
        m_fs = dve.do(lambda e: e.memset(floor_shift[:, :], 0.5 * LN_SHIFT * float(np.log(2.0))), "epsilon")
        act.wait(m_fs)

        def transposed(src, mark):
            ps_n, ps, ps_free = r_small.take()
            pe.wait(mark, ps_free, m_const)
            m_read = pe.do(lambda e: e.transpose(ps[:, 0:P], src, ident), "tile_turned")
            n, xt, free = r_xt.take()
            act.wait(m_read, free)
            m = act.do(lambda e: e.activation(xt[:, :], ps[:, 0:P], ACT.Copy), "tile_copied")
            r_small.done(ps_n, m)
            return n, xt, m, m_read

        def evacuate(ps_n, ps, width, ring_to, mark, sem):
            n, dst, free = ring_to.take()
            flat = dst[:, :] if len(dst.shape) == 2 else dst[:, :, :].rearrange("p a b -> p (a b)")
            act.wait(mark, free)
            m = act.do(lambda e: e.activation(flat[:, 0:width], ps[:, 0:width], ACT.Copy), sem)
            r_big.done(ps_n, m)
            return n, dst, m

        def input_cross(s):
            i = s["tile"]
            n, xn, m = layer_norm(x[:, i, :], x_ready[i])
            s["xt_n"], s["xt"], s["xt_m"], m_read = transposed(xn[:, :], m)
            r_xn.done(n, m_read)

        def input_layer(s):
            i = s["tile"]
            ps_n, ps, ps_free = r_small.take()
            pe.wait(x_ready[i], ps_free)
            pe.do(lambda e: e.matmul(ps[0:64, 0:P], x[:, i, 0:64], ident, start=True, stop=True))
            m = pe.do(lambda e: e.matmul(ps[64:128, 0:P], x[:, i, 64:128], shift, start=True, stop=True),
                      "shifted")
            x_read[i] = [m]
            n, xt, free = r_xt.take()
            act.wait(m, free)
            m = act.do(lambda e: e.activation(xt[:, :], ps[:, 0:P], ACT.Copy), "tile_copied")
            r_small.done(ps_n, m)
            s["xt_n"], s["xt"], s["xt_m"] = n, xt, m

        def project_cross(s, which):
            i, first = s["tile"], s["kind"] == "A"
            n_out = PAIRS if first else 1
            ps_n, ps, free = r_big.take()
            pe.wait(free, s["xt_m"], m_ctx, m_wa if first else m_param)
            if which == "q":
                rhs, k = s["xt"][:, :], D
            else:
                rhs, k = ctx_t[:, i * P:(i + 1) * P], CTX_D
            off = 0 if which == "q" else INNER
            for j in range(n_out):
                lhs = w_in[1][0:k, off + j * P:off + (j + 1) * P] if first else wx[0:k, 0 if which == "q" else 1, :]
                m = pe.do(lambda e, j=j, lhs=lhs: e.matmul(ps[:, j * P:(j + 1) * P], lhs, rhs, start=True, stop=True),
                          "cross_projected" if j == n_out - 1 else None)
            if which == "q":
                r_xt.done(s["xt_n"], m)
            s[which + "_n"], s[which], s[which + "_m"] = evacuate(
                ps_n, ps, n_out * P, r_qt if which == "q" else r_kt, m, which + "_ready")

        def project_cross_v(s):
            i, first = s["tile"], s["kind"] == "A"
            ps_n, ps, free = r_big.take()
            pe.wait(free, m_ctx, m_wa if first else m_param)
            lhs = ctx_t[:, i * P:(i + 1) * P]
            if first:
                for c in range(2):
                    m = pe.do(lambda e, c=c: e.matmul(ps[:, c * 512:(c + 1) * 512], lhs,
                                                      w_in[1][0:CTX_D, 2 * INNER + c * 512:2 * INNER + (c + 1) * 512],
                                                      start=True, stop=True), "v_projected" if c else None)
            else:
                m = pe.do(lambda e: e.matmul(ps[:, 0:D], lhs, wx[0:CTX_D, 2, :], start=True, stop=True), "v_projected")
            s["v_n"], s["v"], s["v_m"] = evacuate(ps_n, ps, INNER if first else D, r_v, m, "v_ready")

        def project_layer(s, which):
            b, col = s["layer"] % 2, {"q": 0, "k": 1, "v": 2}[which]
            ps_n, ps, free = r_big.take()
            pe.wait(free, s["xt_m"], layer_loaded[s["layer"]])
            for c in range(2):
                at = col * INNER + c * 512
                m = pe.do(lambda e, c=c, at=at: e.matmul(ps[:, c * 512:(c + 1) * 512], s["xt"][:, :],
                                                         w_in[b][:, at:at + 512], start=True, stop=True),
                          "rows_projected" if c else None)
            if which == "v":
                r_xt.done(s["xt_n"], m)
                s["v_n"], s["v"], s["v_m"] = evacuate(ps_n, ps, INNER, r_v, m, "v_ready")
                return
            sq_n, sq, sq_free = r_sq.take()
            act.wait(m, sq_free)
            m_sq = act.do(lambda e: e.activation(sq[:, :], ps[:, :], ACT.Square), "squared")
            heads = lambda ap: ap.rearrange("p (h d) -> p h d", d=HEAD_D)
            halves = lambda ap: ap.rearrange("p (h s d) -> p h s d", s=2, d=HEAD_D // 2)
            table = rope[:, s["layer"], 2 * col, None, :].to_broadcast([P, HEADS, HEAD_D])
            sine = rope[:, s["layer"], 2 * col + 1, :].rearrange("p (s d) -> p s d", s=2)[:, None, :, :].to_broadcast(
                [P, HEADS, 2, HEAD_D // 2])
            c_n, cs, c_free = r_cos.take()
            s_n, sn, s_free = r_sin.take()
            dve.wait(m_sq, c_free, s_free, m_rope)
            m_cos = dve.do(lambda e: e.tensor_tensor(heads(cs[:, :]), heads(ps[:, :]), table, ALU.mult), "rotated")
            m_sin = dve.do(lambda e: e.tensor_tensor(halves(sn[:, :]), halves(ps[:, :])[:, :, ::-1, :], sine, ALU.mult),
                           "rotated")
            r_big.done(ps_n, m_sin, m_sq)
            n_n, nm, n_free = r_norm.take()
            dve.wait(n_free, m_sq)
            m = dve.do(lambda e: e.tensor_reduce(nm[:, 0:HEADS], heads(sq[:, :]), AX_X, ALU.add), "norm_summed")
            r_sq.done(sq_n, m)
            dve.wait(m)
            m = dve.do(lambda e: e.tensor_scalar(nm[:, 0:HEADS], nm[:, 0:HEADS], NORM_FLOOR, None, ALU.max),
                       "norm_summed")
            act.wait(m)
            m = act.do(lambda e: e.activation(nm[:, HEADS:2 * HEADS], nm[:, 0:HEADS], ACT.Ln, scale=2.0 ** LN_SHIFT),
                       "log")
            act.wait(m)
            m = act.do(lambda e: e.activation(nm[:, 2 * HEADS:3 * HEADS], nm[:, HEADS:2 * HEADS], ACT.Exp,
                                              bias=floor_shift[:, :], scale=-0.5), "inverse_root")
            pool.wait(m_sin)
            m_add = pool.do(lambda e: e.tensor_tensor(cs[:, :], cs[:, :], sn[:, :], ALU.add), "rotation_added")
            r_sin.done(s_n, m_add)
            pool.wait(m, m_add)
            m = pool.do(lambda e: e.tensor_tensor(
                heads(cs[:, :]), heads(cs[:, :]),
                nm[:, 2 * HEADS:3 * HEADS, None].to_broadcast([P, HEADS, HEAD_D]), ALU.mult), "rows_ready")
            r_norm.done(n_n, m)
            s[which + "_rows"] = (c_n, cs, m)

        def turn(s, which):
            c_n, cs, m_rows = s[which + "_rows"]
            ps_n, ps, free = r_big.take()
            pe.wait(free, m_rows)
            for j in range(PAIRS):
                m = pe.do(lambda e, j=j: e.transpose(ps[:, j * P:(j + 1) * P], cs[:, j * P:(j + 1) * P], ident),
                          "rows_turned" if j == PAIRS - 1 else None)
            r_cos.done(c_n, m)
            s[which + "_n"], s[which], s[which + "_m"] = evacuate(
                ps_n, ps, INNER, r_qt if which == "q" else r_kt, m, which + "_ready")

        def scores(s):
            wide = s["kind"] != "X"
            pairs, hd = (PAIRS, HEAD_D) if wide else (XHEADS // 2, XHEAD_D)
            width, groups = pairs * P, pairs * 2
            masked = s["kind"] == "L"
            step = P if wide else 512
            ps_n, ps, free = r_big.take()
            pe.wait(free, s["q_m"], s["k_m"])
            qt, kt = s["q"], s["k"]
            if masked:
                pe.wait(m_bf)
                for c in range(2):
                    pe.do(lambda e, c=c: e.matmul(ps[:, c * 512:(c + 1) * 512], ident_b[:, :], mask_b[:, :],
                                                  start=True, stop=False, skip_group_check=True))
            for n in range(pairs):
                for b in range(2):
                    for h in range(2):
                        j = (n + h * (pairs // 2)) % pairs if wide else n
                        if wide:
                            lo, jj = h * hd, j
                        else:
                            lo, jj = (2 * j + h) * hd, 0
                        last = n == pairs - 1 and b == 1 and h == 1
                        m = pe.do(lambda e, j=j, b=b, h=h, lo=lo, jj=jj: e.matmul(
                            ps[h * 64:h * 64 + 64, j * step + b * SEQ:j * step + (b + 1) * SEQ],
                            qt[lo:lo + hd, jj, b * SEQ:(b + 1) * SEQ], kt[lo:lo + hd, jj, b * SEQ:(b + 1) * SEQ],
                            start=not masked, stop=True, skip_group_check=masked), "scored" if last else None)
            r_qt.done(s["q_n"], m)
            r_kt.done(s["k_n"], m)
            scale = {"A": HEAD_D ** -0.5, "X": XHEAD_D ** -0.5, "L": 8.0}[s["kind"]]
            grouped = lambda ap: ap[:, 0:width].rearrange("p (g k) -> p g k", k=SEQ)
            p_n, p, p_free = r_p.take()
            t_n, sm, t_free = r_soft.take()
            score = ps[:, :].rearrange("p (j c) -> p j c", c=step)[:, 0:pairs, 0:P].rearrange(
                "p j (b k) -> p j b k", k=SEQ)
            by_pair = lambda ap: ap.rearrange("p (j b) -> p j b", b=2)
            dve.wait(m, t_free, p_free)
            m = dve.do(lambda e: e.tensor_reduce(by_pair(sm[:, 0:groups]), score, AX_X, ALU.max), "row_max")
            dve.wait(m)
            m = dve.do(lambda e: e.tensor_tensor(
                p[:, 0:width].rearrange("p (j b k) -> p j b k", b=2, k=SEQ), score,
                by_pair(sm[:, 0:groups])[:, :, :, None].to_broadcast([P, pairs, 2, SEQ]), ALU.subtract),
                "max_subtracted")
            r_big.done(ps_n, m)
            act.wait(m)
            m = act.do(lambda e: e.activation(p[:, 0:width], p[:, 0:width], ACT.Exp, scale=scale), "exponentials")
            s["soft"] = (p_n, p, t_n, sm, m, width, groups)

        def normalize(s):
            p_n, p, t_n, sm, m, width, groups = s["soft"]
            grouped = lambda ap: ap[:, 0:width].rearrange("p (g k) -> p g k", k=SEQ)
            dve.wait(m)
            m = dve.do(lambda e: e.tensor_reduce(sm[:, HEADS:HEADS + groups], grouped(p), AX_X, ALU.add), "row_sum")
            dve.wait(m)
            m = dve.do(lambda e: e.reciprocal(sm[:, 2 * HEADS:2 * HEADS + groups], sm[:, HEADS:HEADS + groups]),
                       "row_sum")
            pool.wait(m)
            m = pool.do(lambda e: e.tensor_tensor(
                grouped(p), grouped(p), sm[:, 2 * HEADS:2 * HEADS + groups, None].to_broadcast([P, groups, SEQ]),
                ALU.mult), "probabilities")
            r_soft.done(t_n, m)
            s["p_m"] = m

        def turn_probabilities(s):
            p_n, p, width = s["soft"][0], s["soft"][1], s["soft"][5]
            ps_n, ps, free = r_big.take()
            pe.wait(free, s["p_m"])
            for j in range(width // P):
                m = pe.do(lambda e, j=j: e.transpose(ps[:, j * P:(j + 1) * P], p[:, j * P:(j + 1) * P], ident),
                          "probabilities_turned" if j == width // P - 1 else None)
            r_p.done(p_n, m)
            s["pt_n"], s["pt"], s["pt_m"] = evacuate(ps_n, ps, width, r_pt, m, "pt_ready")

        def weigh(s):
            wide = s["kind"] != "X"
            pairs, hd = (PAIRS, HEAD_D) if wide else (XHEADS // 2, XHEAD_D)
            pt, v = s["pt"], s["v"]
            ps_n, ps, free = r_big.take()
            pe.wait(free, s["pt_m"], s["v_m"])
            for n in range(pairs):
                for h in range(2):
                    for b in range(2):
                        j = n
                        head = 2 * j + h
                        lo, at = (h * hd, b * 512 + j * SEQ) if wide else (head * hd, b * 512)
                        last = n == pairs - 1 and h == 1 and b == 1
                        m = pe.do(lambda e, j=j, b=b, h=h, head=head, lo=lo, at=at: e.matmul(
                            ps[lo:lo + hd, at:at + SEQ],
                            v[b * SEQ:(b + 1) * SEQ, head * hd:(head + 1) * hd],
                            pt[b * SEQ:(b + 1) * SEQ, j * P + h * SEQ:j * P + (h + 1) * SEQ],
                            start=True, stop=True), "weighed" if last else None)
            r_pt.done(s["pt_n"], m)
            r_v.done(s["v_n"], m)
            n_out = PAIRS if wide else 1
            s["o_n"], o, free = r_ot.take()
            s["o"] = o
            act.wait(m, free)
            s["o_m"] = act.do(lambda e: e.activation(
                o[:, 0:n_out, :].rearrange("p j (b q) -> p b j q", q=SEQ), ps[:, :].rearrange("p (b j q) -> p b j q", b=2, q=SEQ)[:, :, 0:n_out, :], ACT.Copy),
                "heads_ready")
            r_big.done(ps_n, s["o_m"])

        def output(s):
            i, kind = s["tile"], s["kind"]
            o = s["o"]
            ps_n, ps, free = r_small.take()
            pe.wait(free, s["o_m"], m_const, m_param)
            if kind != "L":
                at = R_BO0 if kind == "A" else R_BO1
                pe.do(lambda e: e.matmul(ps[:, 0:D], ones_row, rows[:, at:at + D], start=True, stop=False))
            n_in = 1 if kind == "X" else PAIRS
            for j in range(n_in):
                w = {"A": lambda j: w_out[1][:, j, :], "X": lambda j: wx[:, 3, :],
                     "L": lambda j: w_out[s["layer"] % 2][:, j, :]}[kind](j)
                m = pe.do(lambda e, j=j, w=w: e.matmul(ps[:, 0:D], o[:, j, :], w, start=(j == 0 and kind == "L"),
                                                       stop=(j == n_in - 1)), "output_projected" if j == n_in - 1 else None)
            r_ot.done(s["o_n"], m)
            dve.wait(m, x_read[i], x_ready[i])
            x_ready[i] = dve.do(lambda e: e.tensor_tensor(x[:, i, :], x[:, i, :], ps[:, 0:D], ALU.add), "x_updated")
            r_small.done(ps_n, x_ready[i])
            if kind == "X":
                pool.wait(x_ready[i])
                m_kept = pool.do(lambda e: e.tensor_copy(x_in[:, i, :], x[:, i, :]), "x_kept")
                dve.wait(m_kept)
                x_ready[i] = layer_norm(x[:, i, :], x_ready[i], place=x[:, i, :])[2]
            s["done"] = m

        def ff_input(g, k):
            i = g["tiles"][k]
            ps_n, ps, free = r_small.take()
            pe.wait(x_ready[i], free)
            m = pe.do(lambda e: e.matmul(ps[:, 0:64], shift, x[:, i, 64:128], start=True, stop=True), "shifted")
            x_read[i] = [m]
            n, xs, xs_free = r_xs.take()
            dve.wait(m, xs_free)
            m1 = dve.do(lambda e: e.tensor_copy(xs[:, 64:128], ps[:, 0:64]), "shifted_rows")
            m2 = dve.do(lambda e: e.tensor_copy(xs[:, 0:64], x[:, i, 0:64]), "shifted_rows")
            r_small.done(ps_n, m1)
            xn_n, xn, m = layer_norm(xs[:, :], m2)
            r_xs.done(n, m)
            g["xn"] = (xn_n, xn, m)

        def ff_turn(g, k):
            xn_n, xn, m = g["xn"]
            layer = g["layer"]
            ps_n, ps, free = r_small.take()
            pe.wait(m, free)
            m = pe.do(lambda e: e.transpose(ps[:, 0:P], xn[:, :], ident), "tile_turned")
            r_xn.done(xn_n, m)
            if k == 0:
                g["fx_n"], g["fx"], g["fx_free"] = r_ffx.take()
            act.wait(m, g["fx_free"], m_param)
            fx = g["fx"]
            g["fx_m"] = act.do(lambda e: e.activation(
                fx[:, k * P:(k + 1) * P], ps[:, 0:P], ACT.Identity, bias=cols[:, B_LNB + layer:B_LNB + layer + 1],
                scale=cols[:, B_LNG + layer:B_LNG + layer + 1]), "tile_copied")
            r_small.done(ps_n, g["fx_m"])

        def ff_hidden(g):
            layer = g["layer"]
            b = layer % 2
            g["h_n"], hid, h_free = r_hid.take()
            g["h"] = hid
            for c in range(FF_CHUNKS):
                ps_n, ps, free = r_big.take()
                pe.wait(free, g["fx_m"], layer_loaded[layer])
                pe.do(lambda e, c=c, ps=ps: e.matmul(ps[:, 0:512], w_ff1[b][:, FF_CHUNKS + c, :], g["fx"][:, :],
                                                     start=True, stop=True))
                m = pe.do(lambda e, c=c, ps=ps: e.matmul(ps[:, 512:1024], w_ff1[b][:, c, :], g["fx"][:, :],
                                                         start=True, stop=True), "hidden_projected")
                at = B_FF1 + 2 * FF_CHUNKS * layer + c
                g_n, gate, g_free = r_gate.take()
                act.wait(m, g_free)
                m_g = act.do(lambda e, ps=ps, at=at, gate=gate: e.activation(
                    gate[:, :], ps[:, 0:512], ACT.Gelu,
                    bias=cols[:, at + FF_CHUNKS:at + FF_CHUNKS + 1]), "gated")
                dve.wait(m_g, h_free)
                g["h_m"] = dve.do(lambda e, ps=ps, at=at, gate=gate, c=c: e.scalar_tensor_tensor(
                    out=hid[:, c, :], in0=ps[:, 512:1024], scalar=cols[:, at:at + 1], in1=gate[:, :],
                    op0=ALU.add, op1=ALU.mult), "hidden_ready")
                r_gate.done(g_n, g["h_m"])
                r_big.done(ps_n, g["h_m"])
            r_ffx.done(g["fx_n"], m)

        def ff_output(g, k):
            layer, i, hid = g["layer"], g["tiles"][k], g["h"]
            ps_n, ps, free = r_small.take()
            pe.wait(free, g["h_m"])
            at = R_FF2 + layer * D
            pe.do(lambda e: e.matmul(ps[:, 0:D], ones_row, rows[:, at:at + D], start=True, stop=False))
            for c in range(FF_CHUNKS):
                m = pe.do(lambda e, c=c: e.matmul(ps[:, 0:D], hid[:, c, k * P:(k + 1) * P], w_ff2[layer % 2][:, c, :],
                                                  start=False, stop=(c == FF_CHUNKS - 1)),
                          "ff_projected" if c == FF_CHUNKS - 1 else None)
            dve.wait(m, x_read[i])
            x_ready[i] = dve.do(lambda e: e.tensor_tensor(x[:, i, :], x[:, i, :], ps[:, 0:D], ALU.add), "x_updated")
            r_small.done(ps_n, x_ready[i])
            if k == GROUP - 1:
                r_hid.done(g["h_n"], m)
            return m

        r_xs = ring("xs", 2, [P, D])

        logits = sb("logits", [P, TILES, EXPERTS])
        onehot = sb("onehot", [P, TILES, EXPERTS])
        onehot_b = sb("onehot_b", [P, TILES, EXPERTS], BF16)
        top = sb("top", [P, 8, TILES])
        slot = sb("slot", [P, 2, TILES], I32)
        r_w1 = ring("moe_w1", 3, [P, HIDDEN])
        r_w2 = ring("moe_w2", 3, [P, HIDDEN // P, D])
        r_row = ring("moe_row", 2, [P, D])
        zeros_n, zeros_buf, _ = r_hid.take()
        zeros = zeros_buf[:, 0:2, :].rearrange("p a b -> p (a b)")
        dispatched = t["dispatched"]
        answers = t["answers"]

        m_z = pool.do(lambda e: e.memset(zeros, 0.0), "zeros")
        sp.wait(m_z)
        d_v = dispatched.rearrange("(h p s) d -> h p (s d)", h=2, p=P)
        for h in range(2):
            m_clear = sp.do(lambda e, h=h: e.dma_start(d_v[h], zeros), "dispatch_cleared", 16)
        m_zero_row = sp.do(lambda e: e.dma_start(answers[SLOTS:SLOTS + 1, :], zeros_buf[0:1, 0, 0:D]), "zero_row", 16)
        r_hid.done(zeros_n, m_clear, m_zero_row)

        expert_w = {}

        def load_expert(e_id):
            n1, w1, free1 = r_w1.take()
            n2, w2, free2 = r_w2.take()
            sp.wait(free1, free2)
            sem = f"expert_weights{n1}"
            sp.do(lambda e: e.dma_start(w1[:, :], t["mw1"][e_id]), sem, 16)
            m = sp.do(lambda e: e.dma_start(w2[:, :, :], t["mw2"][e_id].rearrange("(c p) d -> p c d", p=P)), sem, 16)
            expert_w[e_id] = (n1, w1, n2, w2, m)

        for e_id in range(3):
            load_expert(e_id)

        def routed():
            lg_n, lg, lg_free = r_big.take()
            lgv = lg[:, 0:TILES * EXPERTS].rearrange("p (t e) -> p t e", e=EXPERTS)
            kept = []
            for i in range(TILES):
                n, xn, m = layer_norm(x[:, i, :], x_ready[i])
                xt_n, xt, m_t, m_read = transposed(xn[:, :], m)
                pool.wait(m)
                m_keep = pool.do(lambda e, i=i, xn=xn: e.tensor_copy(x_in[:, i, :], xn[:, :]), "token_kept")
                r_xn.done(n, m_read, m_keep)
                kept.append(m_keep)
                pe.wait(m_t, lg_free if i == 0 else None, m_param)
                pe.do(lambda e, i=i, xt=xt: e.matmul(lgv[:, i, :], xt[:, :], wg[:, :], start=True, stop=False))
                m_l = pe.do(lambda e, i=i: e.matmul(lgv[:, i, :], ones_row, rows[:, R_BG:R_BG + EXPERTS],
                                                    start=False, stop=True), "logits_ready")
                r_xt.done(xt_n, m_l)

            def chain(fn, *marks):
                dve.wait(*marks)
                m = dve.do(fn, "routing")
                dve.wait(m)
                return m

            whole = [P, TILES, EXPERTS]
            spread = lambda n: top[:, n, :, None].to_broadcast(whole)
            expert = const[:, C_EXPERT:C_EXPERT + EXPERTS]
            experts = expert[:, None, :].to_broadcast(whole)
            chain(lambda e: e.tensor_reduce(top[:, 0, :], lgv, AX_X, ALU.max), m_l)
            m = chain(lambda e: e.tensor_tensor(logits[:, :, :], lgv, spread(0), ALU.subtract))
            r_big.done(lg_n, m)
            act.wait(m)
            m_e = act.do(lambda e: e.activation(onehot[:, :, :], logits[:, :, :], ACT.Exp), "gate_exponentials")
            chain(lambda e: e.tensor_reduce(top[:, 1, :], onehot[:, :, :], AX_X, ALU.add), m_e)
            chain(lambda e: e.reciprocal(top[:, 2, :], top[:, 1, :]))
            chain(lambda e: e.tensor_scalar(logits[:, :, :], logits[:, :, :], 0.0, -64.0, ALU.is_ge, ALU.mult))
            chain(lambda e: e.tensor_tensor(logits[:, :, :], logits[:, :, :], experts, ALU.add))
            chain(lambda e: e.tensor_reduce(top[:, 3, :], logits[:, :, :], AX_X, ALU.min))
            chain(lambda e: e.tensor_scalar(top[:, 3, :], top[:, 3, :], 64.0, None, ALU.add))
            chain(lambda e: e.tensor_tensor(onehot[:, :, :], experts, spread(3), ALU.is_equal))
            m = chain(lambda e: e.tensor_copy(onehot_b[:, :, :], onehot[:, :, :]))
            ps_n, ps, free = r_small.take()
            pv = ps[:, 0:TILES * EXPERTS].rearrange("p (t e) -> p t e", e=EXPERTS)
            pe.wait(m, free, m_bf)
            pe.do(lambda e: e.matmul(pv, tri_b[:, :], onehot_b[:, :, :], start=True, stop=True))
            for i in range(TILES - 1):
                rest = TILES - 1 - i
                m = pe.do(lambda e, i=i, rest=rest: e.matmul(
                    pv[:, i + 1:, :], ones_b[:, :], onehot_b[:, i:i + 1, :].to_broadcast([P, rest, EXPERTS]),
                    start=False, stop=True, skip_group_check=True), "earlier_counted" if rest == 1 else None)
            chain(lambda e: e.tensor_tensor(logits[:, :, :], pv, onehot[:, :, :], ALU.mult), m)
            m = chain(lambda e: e.tensor_reduce(top[:, 4, :], logits[:, :, :], AX_X, ALU.add))
            r_small.done(ps_n, m)
            chain(lambda e: e.tensor_scalar(top[:, 5, :], top[:, 3, :], float(CAP), None, ALU.mult))
            chain(lambda e: e.tensor_tensor(top[:, 5, :], top[:, 5, :], top[:, 4, :], ALU.add))
            chain(lambda e: e.tensor_scalar(top[:, 6, :], top[:, 4, :], float(CAP), float(2 * SLOTS),
                                            ALU.is_ge, ALU.mult))
            chain(lambda e: e.tensor_tensor(top[:, 5, :], top[:, 5, :], top[:, 6, :], ALU.add))
            chain(lambda e: e.tensor_copy(slot[:, 0, :], top[:, 5, :]))
            chain(lambda e: e.tensor_scalar(top[:, 7, :], top[:, 5, :], float(SLOTS), None, ALU.min))
            m = chain(lambda e: e.tensor_copy(slot[:, 1, :], top[:, 7, :]))
            pool.wait(m, m_clear)
            for i in range(TILES):
                pool.wait(kept[i])
                m_disp = pool.do(lambda e, i=i: e.indirect_dma_start(
                    out=dispatched, out_offset=bass.IndirectOffsetOnAxis(ap=slot[:, 0, i:i + 1], axis=0),
                    in_=x_in[:, i, :], in_offset=None, bounds_check=SLOTS - 1, oob_is_err=False), "dispatched", 16)
            m_ans = []
            sp.wait(m_disp)
            rows_in = {}

            def load_rows(e_id):
                n, xr, free = r_row.take()
                sp.wait(free)
                rows_in[e_id] = (n, xr, sp.do(lambda e: e.dma_start(xr[:, :], dispatched[e_id * CAP:(e_id + 1) * CAP, :]),
                                              f"slots_loaded{n}", 16))

            load_rows(0)
            for x_id in range(EXPERTS):
                if x_id + 1 < EXPERTS:
                    load_rows(x_id + 1)
                n, xr, m = rows_in[x_id]
                n1, w1, n2, w2, m_w = expert_w[x_id]
                xt_n, xt, m_t, m_read = transposed(xr[:, :], m)
                r_row.done(n, m_read)
                ps_n, ps, free = r_big.take()
                pe.wait(free, m_t, m_w)
                for c in range(HIDDEN // P):
                    m = pe.do(lambda e, c=c, ps=ps, w1=w1, xt=xt: e.matmul(
                        ps[:, c * P:(c + 1) * P], w1[:, c * P:(c + 1) * P], xt[:, :], start=True, stop=True),
                        "expert_hidden" if c == HIDDEN // P - 1 else None)
                r_w1.done(n1, m)
                r_xt.done(xt_n, m)
                h_n, hb, h_free = r_sq.take()
                act.wait(m, h_free)
                for c in range(HIDDEN // P):
                    at = B_MOE1 + x_id * (HIDDEN // P) + c
                    m = act.do(lambda e, c=c, ps=ps, hb=hb, at=at: e.activation(
                        hb[:, c * P:(c + 1) * P], ps[:, c * P:(c + 1) * P], ACT.Relu, bias=cols[:, at:at + 1]),
                        "expert_relu")
                r_big.done(ps_n, m)
                ps_n, ps, free = r_small.take()
                pe.wait(free, m)
                at = R_MOE2 + x_id * D
                pe.do(lambda e, ps=ps, at=at: e.matmul(ps[:, 0:D], ones_row, rows[:, at:at + D], start=True, stop=False))
                for c in range(HIDDEN // P):
                    m = pe.do(lambda e, c=c, ps=ps, hb=hb, w2=w2: e.matmul(
                        ps[:, 0:D], hb[:, c * P:(c + 1) * P], w2[:, c, :], start=False, stop=(c == HIDDEN // P - 1)),
                        "expert_output" if c == HIDDEN // P - 1 else None)
                r_w2.done(n2, m)
                r_sq.done(h_n, m)
                y_n, y, y_free = r_xn.take()
                dve.wait(m, y_free)
                m = dve.do(lambda e, y=y, ps=ps: e.tensor_copy(y[:, :], ps[:, 0:D]), "answer_copied")
                r_small.done(ps_n, m)
                act.wait(m)
                m = act.do(lambda e, x_id=x_id, y=y: e.dma_start(answers[x_id * CAP:(x_id + 1) * CAP, :], y[:, :]),
                           f"answer_stored{y_n}", 16)
                r_xn.done(y_n, m)
                m_ans.append(m)
                if x_id + 3 < EXPERTS:
                    load_expert(x_id + 3)
            pool.wait(m_ans[-1], m_ans[-2], m_zero_row)
            for i in range(TILES):
                n, y, free = r_back.take()
                pool.wait(free)
                m = pool.do(lambda e, i=i, y=y: e.indirect_dma_start(
                    out=y[:, :], out_offset=None, in_=answers,
                    in_offset=bass.IndirectOffsetOnAxis(ap=slot[:, 1, i:i + 1], axis=0),
                    bounds_check=SLOTS, oob_is_err=False), f"answer_fetched{n}", 16)
                dve.wait(m)
                x_ready[i] = dve.do(lambda e, i=i, y=y: e.scalar_tensor_tensor(
                    out=x[:, i, :], in0=y[:, :], scalar=top[:, 2, i:i + 1], in1=x[:, i, :],
                    op0=ALU.mult, op1=ALU.add), "x_updated")
                r_back.done(n, x_ready[i])

        r_back = ring("back", 4, [P, D])

        def run_cross(kind):
            flight = {}
            for step in range(TILES + 2):
                a, b, c = flight.get(step - 2), flight.get(step - 1), None
                if step < TILES:
                    c = flight[step] = {"kind": kind, "tile": step}
                if a:
                    turn_probabilities(a)
                if c:
                    input_cross(c)
                if b:
                    scores(b)
                if a:
                    weigh(a)
                if c:
                    project_cross(c, "k")
                if b:
                    normalize(b)
                if c:
                    project_cross(c, "q")
                if a:
                    output(a)
                if c:
                    project_cross_v(c)
            return a["done"]

        m_first = run_cross("A")
        routed()
        layer_free[1] = [m_first]
        load_layer(1)
        run_cross("X")

        items = [{"kind": "L", "layer": n, "tile": i} for n in range(DEPTH) for i in range(TILES)]
        groups = [{"layer": n, "tiles": list(range(g * GROUP, (g + 1) * GROUP))}
                  for n in range(DEPTH) for g in range(TILES // GROUP)]
        for step in range(len(items) + 2 + GROUP):
            a = items[step - 2] if 2 <= step < len(items) + 2 else None
            b = items[step - 1] if 1 <= step < len(items) + 1 else None
            c = items[step] if step < len(items) else None
            ready = step - 2 - GROUP
            g, k = (groups[ready // GROUP], ready % GROUP) if ready >= 0 else (None, None)
            if a:
                turn_probabilities(a)
            if g and k == 0:
                for kk in range(GROUP):
                    ff_input(g, kk)
                    ff_turn(g, kk)
            if c:
                input_layer(c)
            if b:
                turn(b, "q")
            if a:
                weigh(a)
            if b:
                turn(b, "k")
            if c:
                project_layer(c, "q")
            if a:
                output(a)
            if b:
                scores(b)
            if c:
                project_layer(c, "k")
            if g and k == 1:
                ff_hidden(g)
            if b:
                normalize(b)
            if c:
                project_layer(c, "v")
            if g and k == 2:
                for kk in range(GROUP):
                    m = ff_output(g, kk)
                if g["tiles"][-1] == TILES - 1 and g["layer"] + 2 < DEPTH:
                    layer_free[g["layer"] % 2] = [m]
                    load_layer(g["layer"] + 2)
                if g["layer"] == DEPTH - 1:
                    for i in g["tiles"]:
                        pool.wait(x_ready[i])
                        m = pool.do(lambda e, i=i: e.tensor_tensor(x_in[:, i, :], x_in[:, i, :], x[:, i, :], ALU.add),
                                    "result_ready")
                    sp.wait(m)
                    a0, b0 = g["tiles"][0], g["tiles"][-1] + 1
                    m_out = sp.do(lambda e, a0=a0, b0=b0: e.dma_start(
                        out.rearrange("(t p) d -> p t d", p=P)[:, a0:b0, :], x_in[:, a0:b0, :]), "stored", 16)
        sp.wait(m_out)

        sems = {name: ctx.enter_context(nc.semaphore(name)) for name in counts}
        block = ctx.enter_context(nc.Block())

        @block.sync
        def _(e):
            sp.play(e, sems)

        @block.scalar
        def _(e):
            act.play(e, sems)

        @block.gpsimd
        def _(e):
            pool.play(e, sems)

        @block.vector
        def _(e):
            dve.play(e, sems)

        @block.tensor
        def _(e):
            pe.play(e, sems)


def shape_constants():
    f = np.float32
    c = np.zeros((P, C_END), f)
    tok = np.arange(P)
    c[:, C_IDENT:C_IDENT + P] = np.eye(P)
    c[:, C_SHIFT:C_SHIFT + P] = (tok[:, None] + 1 == tok[None, :]) & (tok[None, :] % SEQ != 0)
    c[:, C_TRI:C_TRI + P] = tok[:, None] < tok[None, :]
    c[:, C_ONES:C_ONES + P] = 1.0
    q, k = (tok % SEQ)[:, None], (np.arange(512) % SEQ)[None, :]
    c[:, C_MASK:C_MASK + 512] = np.where((k <= q) & (q <= k + WINDOW), 0.0, MASKED)
    half = np.arange(0, HEAD_D, 2, dtype=f)
    inv_freq = (f(1.0) / (f(10000.0) ** (half / f(HEAD_D)))).astype(f)
    pos = np.arange(SEQ, dtype=f)
    freqs = (pos[:, None] * inv_freq[None, :]).astype(f)
    base = ((half + f(0.4 * HEAD_D)) / f(1.4 * HEAD_D)).astype(f)
    power = ((pos - f(SEQ // 2)) / f(WINDOW // 2)).astype(f)
    scale = (base[None, :] ** power[:, None]).astype(f)
    cos, sin = np.cos(freqs).astype(f), np.sin(freqs).astype(f)
    for s, sc in enumerate((scale, f(1.0) / scale)):
        block = np.concatenate([cos * sc, cos * sc, -sin * sc, sin * sc], 1)
        c[:, C_ROPE + 2 * s * HEAD_D:C_ROPE + 2 * (s + 1) * HEAD_D] = np.tile(block, (2, 1))
    c[:, C_EXPERT:C_EXPERT + EXPERTS] = np.arange(EXPERTS)
    return c


def kernel(**inputs):
    import concourse.bacc as bacc
    from concourse.bass_utils import run_bass_kernel_spmd

    v = {k: np.ascontiguousarray(a) for k, a in inputs.items()}
    chunks = 2 * FF_CHUNKS
    ff1 = np.zeros((DEPTH, D, 2, FF_CHUNKS * P), np.float32)
    ff1[:, :, :, :FF] = v["L1_ffn_W1"].reshape(DEPTH, D, 2, FF)
    ffb = np.zeros((DEPTH, 2, FF_CHUNKS * P), np.float32)
    ffb[:, :, :FF] = v["L1_ffn_b1"].reshape(DEPTH, 2, FF)
    ff2 = np.zeros((DEPTH, FF_CHUNKS * P, D), np.float32)
    ff2[:, :FF] = v["L1_ffn_W2"]
    cols = np.concatenate([
        v["L0_ffn_b1"].reshape(EXPERTS * HIDDEN // P, P).T,
        ffb.reshape(DEPTH * chunks, P).T, v["L1_ffn_ln_g"].T, v["L1_ffn_ln_b"].T], 1)
    rows = np.concatenate([v["L0_xattn_bo"], v["L0_ffn_bg"], v["L0_ffn_b2"].reshape(-1), v["L1_xattn_bo"],
                           v["L1_ffn_b2"].reshape(-1)])[None]
    wx = np.zeros((P, 4, D), np.float32)
    for n, name in enumerate(("Wq", "Wk", "Wv", "Wo")):
        w = v["L1_xattn_" + name].T
        wx[:w.shape[0], n] = w
    arrays = {
        "const": shape_constants(),
        "x": v["x"].reshape(-1, D),
        "ctx_t": np.ascontiguousarray(v["ctx_768"].reshape(-1, CTX_D).T),
        "wq": v["L0_xattn_Wq"], "wk": v["L0_xattn_Wk"], "wv": v["L0_xattn_Wv"], "wo": v["L0_xattn_Wo"],
        "cols": np.ascontiguousarray(cols), "rows": np.ascontiguousarray(rows), "wx": wx,
        "wg": v["L0_ffn_Wg"],
        "scales": np.stack([v["L1_ffn_q_scale"], v["L1_ffn_k_scale"]])[None],
        "wqkv": v["L1_ffn_Wqkv"], "lwo": v["L1_ffn_Wo"],
        "ff1": ff1.reshape(DEPTH, D, chunks, P), "ff2": ff2,
        "mw1": v["L0_ffn_W1"], "mw2": v["L0_ffn_W2"],
    }
    nc = bacc.Bacc("TRN2", target_bir_lowering=False, num_devices=1)
    t = {name: nc.dram_tensor(name + "_dram", a.shape, mybir.dt.from_np(a.dtype), kind="ExternalInput").ap()
         for name, a in arrays.items()}
    t["dispatched"] = nc.dram_tensor("dispatched", [SLOTS, D], F32, kind="Internal").ap()
    t["answers"] = nc.dram_tensor("answers", [SLOTS + 1, D], F32, kind="Internal").ap()
    out = nc.dram_tensor("out_dram", [BATCH * SEQ, D], F32, kind="ExternalOutput").ap()
    build(nc, t, out)
    r = run_bass_kernel_spmd(nc, [{name + "_dram": a for name, a in arrays.items()}], core_ids=[0])
    return r.results[0]["out_dram"].reshape(BATCH, SEQ, D)
```

```python
from contextlib import ExitStack

import numpy as np

import concourse.bass as bass
from concourse import mybir

F32 = mybir.dt.float32
BF16 = mybir.dt.bfloat16
I32 = mybir.dt.int32
ALU = mybir.AluOpType
ACT = mybir.ActivationFunctionType
AX_X = mybir.AxisListType.X

P = 128
D = 128
BATCH, SEQ = 32, 64
TILES = BATCH * SEQ // P
CTX_D = 96
HEADS, HEAD_D = 16, 64
INNER = HEADS * HEAD_D
PAIRS = HEADS // 2
XHEADS, XHEAD_D = 4, 32
EXPERTS, HIDDEN = 16, 512
CAP = BATCH * SEQ // EXPERTS
SLOTS = EXPERTS * CAP
DEPTH = 6
WINDOW = 32
FF = D * 4 * 2 // 3
FF_CHUNKS = 3
GROUP = 4
LN_EPS = 1e-5
NORM_FLOOR = 1e-24
LN_SHIFT = 17
MASKED = -1e30

C_IDENT, C_SHIFT, C_TRI, C_ONES, C_MASK = 0, 128, 256, 384, 512
C_ROPE, C_EXPERT, C_END = 1024, 1280, 1296
B_MOE1, B_FF1, B_LNG, B_LNB, B_END = 0, 64, 100, 106, 112
R_BO0, R_BG, R_BO1, R_FF2, R_END = 0, 128, 144, 272, 1040


class Mark:

    def __init__(self, sem, value):
        self.sem, self.value = sem, value


class Queue:

    def __init__(self, counts):
        self.steps, self.waited, self.counts = [], {}, counts

    def wait(self, *marks):
        for m in marks:
            if isinstance(m, (list, tuple)):
                self.wait(*m)
            elif m is not None and self.waited.get(m.sem, 0) < m.value:
                self.waited[m.sem] = m.value
                self.steps.append((None, m.sem, m.value))

    def do(self, instruction, sem=None, by=1):
        self.steps.append((instruction, sem, by))
        if sem is None:
            return None
        self.counts[sem] = self.counts.get(sem, 0) + by
        return Mark(sem, self.counts[sem])

    def play(self, engine, sems):
        for instruction, sem, value in self.steps:
            if instruction is None:
                engine.wait_ge(sems[sem], value)
            elif sem is None:
                instruction(engine)
            else:
                instruction(engine).then_inc(sems[sem], value)


class Ring:

    def __init__(self, buffers):
        self.buffers, self.free, self.turn = buffers, [[] for _ in buffers], -1

    def take(self):
        self.turn = (self.turn + 1) % len(self.buffers)
        free, self.free[self.turn] = self.free[self.turn], None
        assert free is not None, "a buffer is taken before its last use is written down"
        return self.turn, self.buffers[self.turn], free

    def done(self, n, *marks):
        self.free[n] = list(marks)


def build(nc, t, out):
    counts = {}
    pe, act, dve, pool, sp = (Queue(counts) for _ in range(5))
    ctx = ExitStack()
    with ctx:
        def sb(name, shape, dt=F32):
            return ctx.enter_context(nc.sbuf_tensor(name, shape, dt))

        x = sb("x", [P, TILES, D])
        x_in = sb("x_in", [P, TILES, D])
        ctx_t = sb("ctx_t", [CTX_D, BATCH * SEQ])
        const = sb("const", [P, C_END])
        cols = sb("cols", [P, B_END])
        rows = sb("rows", [1, R_END])
        scales = sb("scales", [P, 2, DEPTH, HEAD_D])
        rope = sb("rope", [P, DEPTH, 4, HEAD_D])
        mask_b = sb("mask_b", [P, 512], BF16)
        ident_b = sb("ident_b", [P, P], BF16)
        tri_b = sb("tri_b", [P, P], BF16)
        ones_b = sb("ones_b", [P, P], BF16)
        w_in = [sb(f"w_in{n}", [P, 3 * INNER]) for n in range(2)]
        w_out = [sb(f"w_out{n}", [P, PAIRS, D]) for n in range(2)]
        w_ff1 = [sb(f"w_ff1{n}", [P, 2 * FF_CHUNKS, P]) for n in range(2)]
        w_ff2 = [sb(f"w_ff2{n}", [P, FF_CHUNKS, D]) for n in range(2)]
        wx = sb("wx", [P, 4, D])
        wg = sb("wg", [D, EXPERTS])

        def ring(name, n, shape, dt=F32):
            return Ring([sb(f"{name}{i}", shape, dt) for i in range(n)])

        r_stat = ring("stat", 4, [P, 12])
        r_xn = ring("xn", 4, [P, D])
        r_xt = ring("xt", 5, [P, P])
        r_raw = ring("raw", 2, [P, INNER])
        r_sq = ring("sq", 2, [P, INNER])
        r_cos = ring("cos", 4, [P, INNER])
        r_sin = ring("sin", 2, [P, INNER])
        r_norm = ring("norm", 2, [P, 3, 2, HEADS])
        wide_rings = {
            "q": ring("qt", 1, [P, PAIRS, P]), "k": ring("kt", 1, [P, PAIRS, P]), "v": ring("v", 4, [P, INNER]),
            "p": ring("p", 2, [P, INNER]), "pt": ring("pt", 1, [P, INNER]), "ot": ring("ot", 1, [P, PAIRS, P])}
        narrow_rings = {
            "q": ring("xqt", 2, [P, 1, P]), "k": ring("xkt", 2, [P, 1, P]), "v": ring("xv", 3, [P, D]),
            "p": ring("xp", 2, [P, 2 * P]), "pt": ring("xpt", 1, [P, 2 * P]), "ot": ring("xot", 1, [P, 1, P])}
        rings_of = {"A": wide_rings, "L": wide_rings, "X": narrow_rings}
        r_soft = ring("soft", 5, [P, 3 * HEADS])
        r_ffx = ring("ffx", 1, [P, GROUP * P])
        r_gate = ring("gate", 2, [P, GROUP * P])
        r_hid = ring("hid", 1, [P, FF_CHUNKS, GROUP * P])
        r_big = Ring([ctx.enter_context(nc.psum_tensor(f"big{i}", [P, 1024], F32)) for i in range(3)])
        r_small = Ring([ctx.enter_context(nc.psum_tensor(f"small{i}", [P, 512], F32)) for i in range(2)])

        ident = const[:, C_IDENT:C_IDENT + P]
        shift = const[:, C_SHIFT:C_SHIFT + P]
        ones_row = const[0:1, C_ONES:C_ONES + P]

        m_const = sp.do(lambda e: e.dma_start(const[:, :], t["const"]), "const_loaded", 16)
        x_loaded = []
        x_d = t["x"].rearrange("(t p) d -> p t d", p=P)
        for q in range(4):
            a, b = 4 * q, 4 * q + 4
            x_loaded += 4 * [sp.do(lambda e, a=a, b=b: e.dma_start(x[:, a:b, :], x_d[:, a:b, :]),
                                   f"x_loaded{q}", 16)]
        for n, name in enumerate(("wq", "wk", "wv")):
            k = D if n == 0 else CTX_D
            m_wa = sp.do(lambda e, n=n, k=k, name=name: e.dma_start(
                w_in[1][0:k, n * INNER:(n + 1) * INNER], t[name]), "first_weights", 16)
        m_wa = sp.do(lambda e: e.dma_start(
            w_out[1][:, :, :], t["wo"].rearrange("(j p) n -> p j n", p=P)), "first_weights", 16)
        m_ctx = sp.do(lambda e: e.dma_start(ctx_t[:, :], t["ctx_t"]), "context_loaded", 16)
        for dst, src in ((cols[:, :], t["cols"]), (rows[:, :], t["rows"]), (wx[:, :, :], t["wx"]),
                         (wg[:, :], t["wg"]), (scales[:, :, :, :], t["scales"].to_broadcast([P, 2, DEPTH, HEAD_D]))):
            m_param = sp.do(lambda e, dst=dst, src=src: e.dma_start(dst, src), "parameters_loaded", 16)

        layer_free = [[], []]
        layer_loaded = {}

        def load_layer(n):
            b = n % 2
            sp.wait(layer_free[b])
            sem = f"layer_weights{b}"
            sp.do(lambda e: e.dma_start(w_in[b][:, :], t["wqkv"][n]), sem, 16)
            sp.do(lambda e: e.dma_start(w_out[b][:, :, :], t["lwo"][n].rearrange("(j p) n -> p j n", p=P)), sem, 16)
            sp.do(lambda e: e.dma_start(w_ff1[b][:, :, :], t["ff1"][n]), sem, 16)
            layer_loaded[n] = sp.do(lambda e: e.dma_start(
                w_ff2[b][:, :, :], t["ff2"][n].rearrange("(c p) n -> p c n", p=P)), sem, 16)

        load_layer(0)

        dve.wait(m_const)
        for dst, at, n in ((mask_b, C_MASK, 512), (ident_b, C_IDENT, P), (tri_b, C_TRI, P), (ones_b, C_ONES, P)):
            m_bf = dve.do(lambda e, dst=dst, at=at, n=n: e.tensor_copy(dst[:, :], const[:, at:at + n]), "bf16_constants")
        pool.wait(m_const, m_param)
        for n in range(DEPTH):
            for s in range(2):
                base = const[:, C_ROPE + 2 * s * HEAD_D:C_ROPE + 2 * (s + 1) * HEAD_D]
                m_rope = pool.do(lambda e, n=n, s=s, base=base: e.tensor_tensor(
                    rope[:, n, 2 * s, :], base[:, 0:HEAD_D], scales[:, s, n, :], ALU.mult), "rope_tables")
                half = HEAD_D // 2
                for h in range(2):
                    m_rope = pool.do(lambda e, n=n, s=s, base=base, h=h: e.tensor_tensor(
                        rope[:, n, 2 * s + 1, h * half:(h + 1) * half],
                        base[:, HEAD_D + h * half:HEAD_D + (h + 1) * half],
                        scales[:, s, n, (1 - h) * half:(2 - h) * half], ALU.mult), "rope_tables")

        x_ready = list(x_loaded)
        x_read = [[] for _ in range(TILES)]

        exp_tables = lambda: act.do(lambda e: e.preload_act_table_set("natural_log_exp_and_others"))
        exp_tables()

        def norm_factors(src, mark):
            sn, st, sfree = r_stat.take()
            dve.wait(mark, sfree)
            m = dve.do(lambda e: e.bn_stats(st[:, 0:6], src), "norm_stats")
            dve.wait(m)
            m = dve.do(lambda e: e.bn_aggr(st[:, 6:8], st[:, 0:6]), "norm_stats")
            act.wait(m)
            m = act.do(lambda e: e.activation(st[:, 8:9], st[:, 7:8], ACT.Ln, bias=st[:, 9:10]), "log")
            act.wait(m)
            m = act.do(lambda e: e.activation(st[:, 8:9], st[:, 8:9], ACT.Exp, scale=-0.5), "inverse_root")
            return sn, st, m

        def layer_norm(src, factors, place=None):
            sn, st, m = factors
            n, xn, free = r_xn.take() if place is None else (None, None, None)
            dve.wait(m, free)
            dst = xn[:, :] if place is None else place
            m = dve.do(lambda e: e.tensor_scalar(dst, src, st[:, 6:7], st[:, 8:9], ALU.subtract, ALU.mult),
                       "normalized")
            r_stat.done(sn, m)
            return n, xn, m

        for st in r_stat.buffers:
            m_eps = dve.do(lambda e, st=st: e.memset(st[:, 9:10], LN_EPS), "epsilon")
        act.wait(m_eps)
        floor_shift = sb("floor_shift", [P, 1])
        m_fs = dve.do(lambda e: e.memset(floor_shift[:, :], 0.5 * LN_SHIFT * float(np.log(2.0))), "epsilon")
        act.wait(m_fs)

        def transposed(src, mark):
            ps_n, ps, ps_free = r_small.take()
            pe.wait(mark, ps_free, m_const)
            m_read = pe.do(lambda e: e.transpose(ps[:, 0:P], src, ident), "tile_turned")
            n, xt, free = r_xt.take()
            act.wait(m_read, free)
            m = act.do(lambda e: e.activation(xt[:, :], ps[:, 0:P], ACT.Copy), "tile_copied")
            r_small.done(ps_n, m)
            return n, xt, m, m_read

        def evacuate(ps_n, ps, width, ring_to, mark, sem):
            n, dst, free = ring_to.take()
            flat = dst[:, :] if len(dst.shape) == 2 else dst[:, :, :].rearrange("p a b -> p (a b)")
            act.wait(mark, free)
            m = act.do(lambda e: e.activation(flat[:, 0:width], ps[:, 0:width], ACT.Copy), sem)
            r_big.done(ps_n, m)
            return n, dst, m

        def input_cross(s):
            i = s["tile"]
            n, xn, m = layer_norm(x[:, i, :], norm_factors(x[:, i, :], x_ready[i]))
            s["xt_n"], s["xt"], s["xt_m"], m_read = transposed(xn[:, :], m)
            r_xn.done(n, m_read)

        def input_layer(s):
            i = s["tile"]
            ps_n, ps, ps_free = r_small.take()
            pe.wait(x_ready[i], ps_free)
            pe.do(lambda e: e.matmul(ps[0:64, 0:P], x[:, i, 0:64], ident, start=True, stop=True))
            m = pe.do(lambda e: e.matmul(ps[64:128, 0:P], x[:, i, 64:128], shift, start=True, stop=True),
                      "shifted")
            x_read[i] = [m]
            n, xt, free = r_xt.take()
            act.wait(m, free)
            m = act.do(lambda e: e.activation(xt[:, :], ps[:, 0:P], ACT.Copy), "tile_copied")
            r_small.done(ps_n, m)
            s["xt_n"], s["xt"], s["xt_m"] = n, xt, m

        def project_cross(s, which):
            i, first = s["tile"], s["kind"] == "A"
            n_out = PAIRS if first else 1
            ps_n, ps, free = r_big.take()
            pe.wait(free, s["xt_m"], m_ctx, m_wa if first else m_param)
            if which == "q":
                rhs, k = s["xt"][:, :], D
            else:
                rhs, k = ctx_t[:, i * P:(i + 1) * P], CTX_D
            off = 0 if which == "q" else INNER
            for j in range(n_out):
                lhs = w_in[1][0:k, off + j * P:off + (j + 1) * P] if first else wx[0:k, 0 if which == "q" else 1, :]
                m = pe.do(lambda e, j=j, lhs=lhs: e.matmul(ps[:, j * P:(j + 1) * P], lhs, rhs, start=True, stop=True),
                          "cross_projected" if j == n_out - 1 else None)
            if which == "q":
                r_xt.done(s["xt_n"], m)
            s[which + "_n"], s[which], s[which + "_m"] = evacuate(
                ps_n, ps, n_out * P, rings_of[s["kind"]][which], m, which + "_ready")

        def project_cross_v(s):
            i, first = s["tile"], s["kind"] == "A"
            ps_n, ps, free = r_big.take()
            pe.wait(free, m_ctx, m_wa if first else m_param)
            lhs = ctx_t[:, i * P:(i + 1) * P]
            if first:
                for c in range(2):
                    m = pe.do(lambda e, c=c: e.matmul(ps[:, c * 512:(c + 1) * 512], lhs,
                                                      w_in[1][0:CTX_D, 2 * INNER + c * 512:2 * INNER + (c + 1) * 512],
                                                      start=True, stop=True), "v_projected" if c else None)
            else:
                m = pe.do(lambda e: e.matmul(ps[:, 0:D], lhs, wx[0:CTX_D, 2, :], start=True, stop=True), "v_projected")
            s["v_n"], s["v"], s["v_m"] = evacuate(ps_n, ps, INNER if first else D, rings_of[s["kind"]]["v"], m, "v_ready")

        def project_layer(s, which):
            b, col = s["layer"] % 2, {"q": 0, "k": 1, "v": 2}[which]
            ps_n, ps, free = r_big.take()
            pe.wait(free, s["xt_m"], layer_loaded[s["layer"]])
            for c in range(2):
                at = col * INNER + c * 512
                m = pe.do(lambda e, c=c, at=at: e.matmul(ps[:, c * 512:(c + 1) * 512], s["xt"][:, :],
                                                         w_in[b][:, at:at + 512], start=True, stop=True),
                          "rows_projected" if c else None)
            if which == "v":
                r_xt.done(s["xt_n"], m)
                s["v_n"], s["v"], s["v_m"] = evacuate(ps_n, ps, INNER, wide_rings["v"], m, "v_ready")
                return
            s[which + "_raw"] = evacuate(ps_n, ps, INNER, r_raw, m, "rows_raw")

        def rotate(s, which):
            col = "qk".index(which)
            raw_n, raw, raw_m = s[which + "_raw"]
            heads = lambda ap: ap.rearrange("p (h d) -> p h d", d=HEAD_D)
            halves = lambda ap: ap.rearrange("p (h s d) -> p h s d", s=2, d=HEAD_D // 2)
            table = rope[:, s["layer"], 2 * col, None, :].to_broadcast([P, HEADS, HEAD_D])
            sine = rope[:, s["layer"], 2 * col + 1, :].rearrange("p (s d) -> p s d", s=2)[:, None, :, :].to_broadcast(
                [P, HEADS, 2, HEAD_D // 2])
            c_n, cs, c_free = r_cos.take()
            s_n, sn, s_free = r_sin.take()
            dve.wait(raw_m, c_free, s_free, m_rope)
            m_cos = dve.do(lambda e: e.tensor_tensor(heads(cs[:, :]), heads(raw[:, :]), table, ALU.mult), "rotated")
            m_sin = dve.do(lambda e: e.tensor_tensor(halves(sn[:, :]), halves(raw[:, :])[:, :, ::-1, :], sine, ALU.mult),
                           "rotated")
            pool.wait(m_sin)
            m_add = pool.do(lambda e: e.tensor_tensor(cs[:, :], cs[:, :], sn[:, :], ALU.add), "rotation_added")
            r_sin.done(s_n, m_add)
            s[which + "_raw"] = (raw_n, raw, raw_m, m_sin)
            s[which + "_rows"] = [c_n, cs, m_add]

        def square(s, which):
            raw_n, raw, raw_m, m_sin = s[which + "_raw"]
            sq_n, sq, sq_free = r_sq.take()
            act.wait(raw_m, sq_free)
            m = act.do(lambda e: e.activation(sq[:, :], raw[:, :], ACT.Square), "squared")
            r_raw.done(raw_n, m_sin, m)
            s[which + "_sq"] = (sq_n, sq, m)

        def sum_squares(s, which):
            sq_n, sq, m_sq = s[which + "_sq"]
            col = "qk".index(which)
            if col == 0:
                s["norm"] = r_norm.take()
            nm, n_free = s["norm"][1:]
            dve.wait(n_free, m_sq)
            s["norm_m"] = dve.do(lambda e: e.tensor_reduce(
                nm[:, 0, col, :], sq[:, :].rearrange("p (h d) -> p h d", d=HEAD_D), AX_X, ALU.add), "norm_summed")
            r_sq.done(sq_n, s["norm_m"])

        def inverse_norms(s):
            nm, m = s["norm"][1], s["norm_m"]
            dve.wait(m)
            m = dve.do(lambda e: e.tensor_scalar(nm[:, 0, :, :], nm[:, 0, :, :], NORM_FLOOR, None, ALU.max),
                       "norm_summed")
            act.wait(m)
            m = act.do(lambda e: e.activation(nm[:, 1, :, :], nm[:, 0, :, :], ACT.Ln, scale=2.0 ** LN_SHIFT), "log")
            act.wait(m)
            s["norm_m"] = act.do(lambda e: e.activation(nm[:, 2, :, :], nm[:, 1, :, :], ACT.Exp,
                                                        bias=floor_shift[:, :], scale=-0.5), "inverse_root")

        def scale_rows(s, which):
            c_n, cs, m_add = s[which + "_rows"]
            n_n, nm, _ = s["norm"]
            col = "qk".index(which)
            heads = lambda ap: ap.rearrange("p (h d) -> p h d", d=HEAD_D)
            pool.wait(m_add, s["norm_m"])
            m = pool.do(lambda e: e.tensor_tensor(
                heads(cs[:, :]), heads(cs[:, :]),
                nm[:, 2, col, :, None].to_broadcast([P, HEADS, HEAD_D]), ALU.mult), "rows_ready")
            if col == 1:
                r_norm.done(n_n, m)
            s[which + "_rows"][2] = m

        def turn(s, which):
            c_n, cs, m_rows = s[which + "_rows"]
            ps_n, ps, free = r_big.take()
            pe.wait(free, m_rows)
            for j in range(PAIRS):
                m = pe.do(lambda e, j=j: e.transpose(ps[:, j * P:(j + 1) * P], cs[:, j * P:(j + 1) * P], ident),
                          "rows_turned" if j == PAIRS - 1 else None)
            r_cos.done(c_n, m)
            s[which + "_n"], s[which], s[which + "_m"] = evacuate(
                ps_n, ps, INNER, wide_rings[which], m, which + "_ready")

        def scores(s):
            wide = s["kind"] != "X"
            pairs, hd = (PAIRS, HEAD_D) if wide else (XHEADS // 2, XHEAD_D)
            width, groups = pairs * P, pairs * 2
            masked = s["kind"] == "L"
            rings = rings_of[s["kind"]]
            step = P if wide else 512
            ps_n, ps, free = r_big.take()
            pe.wait(free, s["q_m"], s["k_m"])
            qt, kt = s["q"], s["k"]
            if masked:
                pe.wait(m_bf)
                for c in range(2):
                    pe.do(lambda e, c=c: e.matmul(ps[:, c * 512:(c + 1) * 512], ident_b[:, :], mask_b[:, :],
                                                  start=True, stop=False, skip_group_check=True))
            for n in range(pairs):
                for b in range(2):
                    for h in range(2):
                        j = (n + h * (pairs // 2)) % pairs if wide else n
                        if wide:
                            lo, jj = h * hd, j
                        else:
                            lo, jj = (2 * j + h) * hd, 0
                        last = n == pairs - 1 and b == 1 and h == 1
                        m = pe.do(lambda e, j=j, b=b, h=h, lo=lo, jj=jj: e.matmul(
                            ps[h * 64:h * 64 + 64, j * step + b * SEQ:j * step + (b + 1) * SEQ],
                            qt[lo:lo + hd, jj, b * SEQ:(b + 1) * SEQ], kt[lo:lo + hd, jj, b * SEQ:(b + 1) * SEQ],
                            start=not masked, stop=True, skip_group_check=masked), "scored" if last else None)
            rings["q"].done(s["q_n"], m)
            rings["k"].done(s["k_n"], m)
            scale = {"A": HEAD_D ** -0.5, "X": XHEAD_D ** -0.5, "L": 8.0}[s["kind"]]
            grouped = lambda ap: ap[:, 0:width].rearrange("p (g k) -> p g k", k=SEQ)
            p_n, p, p_free = rings["p"].take()
            t_n, sm, t_free = r_soft.take()
            score = ps[:, :].rearrange("p (j c) -> p j c", c=step)[:, 0:pairs, 0:P].rearrange(
                "p j (b k) -> p j b k", k=SEQ)
            by_pair = lambda ap: ap.rearrange("p (j b) -> p j b", b=2)
            dve.wait(m, t_free, p_free)
            m = dve.do(lambda e: e.tensor_reduce(by_pair(sm[:, 0:groups]), score, AX_X, ALU.max), "row_max")
            dve.wait(m)
            m = dve.do(lambda e: e.tensor_tensor(
                p[:, 0:width].rearrange("p (j b k) -> p j b k", b=2, k=SEQ), score,
                by_pair(sm[:, 0:groups])[:, :, :, None].to_broadcast([P, pairs, 2, SEQ]), ALU.subtract),
                "max_subtracted")
            r_big.done(ps_n, m)
            s["soft"] = (p_n, p, t_n, sm, m, width, groups, scale)

        def exponentials(s):
            p_n, p, t_n, sm, m, width, groups, scale = s["soft"]
            act.wait(m)
            s["exp_m"] = act.do(lambda e: e.activation(p[:, 0:width], p[:, 0:width], ACT.Exp, scale=scale),
                                "exponentials")

        def normalize(s):
            p_n, p, t_n, sm, m, width, groups, _ = s["soft"]
            grouped = lambda ap: ap[:, 0:width].rearrange("p (g k) -> p g k", k=SEQ)
            dve.wait(s["exp_m"])
            m = dve.do(lambda e: e.tensor_reduce(sm[:, HEADS:HEADS + groups], grouped(p), AX_X, ALU.add), "row_sum")
            dve.wait(m)
            m = dve.do(lambda e: e.reciprocal(sm[:, 2 * HEADS:2 * HEADS + groups], sm[:, HEADS:HEADS + groups]),
                       "row_sum")
            pool.wait(m)
            m = pool.do(lambda e: e.tensor_tensor(
                grouped(p), grouped(p), sm[:, 2 * HEADS:2 * HEADS + groups, None].to_broadcast([P, groups, SEQ]),
                ALU.mult), "probabilities")
            r_soft.done(t_n, m)
            s["p_m"] = m

        def turn_probabilities(s):
            p_n, p, width = s["soft"][0], s["soft"][1], s["soft"][5]
            rings = rings_of[s["kind"]]
            ps_n, ps, free = r_big.take()
            pe.wait(free, s["p_m"])
            for j in range(width // P):
                m = pe.do(lambda e, j=j: e.transpose(ps[:, j * P:(j + 1) * P], p[:, j * P:(j + 1) * P], ident),
                          "probabilities_turned" if j == width // P - 1 else None)
            rings["p"].done(p_n, m)
            s["pt_n"], s["pt"], s["pt_m"] = evacuate(ps_n, ps, width, rings["pt"], m, "pt_ready")

        def weigh(s):
            wide = s["kind"] != "X"
            pairs, hd = (PAIRS, HEAD_D) if wide else (XHEADS // 2, XHEAD_D)
            pt, v = s["pt"], s["v"]
            ps_n, ps, free = r_big.take()
            pe.wait(free, s["pt_m"], s["v_m"])
            for n in range(pairs):
                for h in range(2):
                    for b in range(2):
                        j = n
                        head = 2 * j + h
                        lo, at = (h * hd, b * 512 + j * SEQ) if wide else (head * hd, b * 512)
                        last = n == pairs - 1 and h == 1 and b == 1
                        m = pe.do(lambda e, j=j, b=b, h=h, head=head, lo=lo, at=at: e.matmul(
                            ps[lo:lo + hd, at:at + SEQ],
                            v[b * SEQ:(b + 1) * SEQ, head * hd:(head + 1) * hd],
                            pt[b * SEQ:(b + 1) * SEQ, j * P + h * SEQ:j * P + (h + 1) * SEQ],
                            start=True, stop=True), "weighed" if last else None)
            rings = rings_of[s["kind"]]
            rings["pt"].done(s["pt_n"], m)
            rings["v"].done(s["v_n"], m)
            n_out = PAIRS if wide else 1
            s["o_n"], o, free = rings["ot"].take()
            s["o"] = o
            act.wait(m, free)
            s["o_m"] = act.do(lambda e: e.activation(
                o[:, 0:n_out, :].rearrange("p j (b q) -> p b j q", q=SEQ), ps[:, :].rearrange("p (b j q) -> p b j q", b=2, q=SEQ)[:, :, 0:n_out, :], ACT.Copy),
                "heads_ready")
            r_big.done(ps_n, s["o_m"])

        def output(s):
            i, kind = s["tile"], s["kind"]
            o = s["o"]
            ps_n, ps, free = r_small.take()
            pe.wait(free, s["o_m"], m_const, m_param)
            if kind != "L":
                at = R_BO0 if kind == "A" else R_BO1
                pe.do(lambda e: e.matmul(ps[:, 0:D], ones_row, rows[:, at:at + D], start=True, stop=False))
            n_in = 1 if kind == "X" else PAIRS
            for j in range(n_in):
                w = {"A": lambda j: w_out[1][:, j, :], "X": lambda j: wx[:, 3, :],
                     "L": lambda j: w_out[s["layer"] % 2][:, j, :]}[kind](j)
                m = pe.do(lambda e, j=j, w=w: e.matmul(ps[:, 0:D], o[:, j, :], w, start=(j == 0 and kind == "L"),
                                                       stop=(j == n_in - 1)), "output_projected" if j == n_in - 1 else None)
            rings_of[kind]["ot"].done(s["o_n"], m)
            dve.wait(m, x_read[i], x_ready[i])
            x_ready[i] = dve.do(lambda e: e.tensor_tensor(x[:, i, :], x[:, i, :], ps[:, 0:D], ALU.add), "x_updated")
            r_small.done(ps_n, x_ready[i])
            if kind == "X":
                pool.wait(x_ready[i])
                m_kept = pool.do(lambda e: e.tensor_copy(x_in[:, i, :], x[:, i, :]), "x_kept")
                dve.wait(m_kept)
                x_ready[i] = layer_norm(x[:, i, :], norm_factors(x[:, i, :], x_ready[i]), place=x[:, i, :])[2]
            s["done"] = m

        def ff_input(s):
            i = s["tile"]
            ps_n, ps, free = r_small.take()
            pe.wait(x_ready[i], free)
            m = pe.do(lambda e: e.matmul(ps[:, 0:64], shift, x[:, i, 64:128], start=True, stop=True), "shifted")
            x_read[i] = [m]
            n, xs, xs_free = r_xs.take()
            dve.wait(m, xs_free)
            m1 = dve.do(lambda e: e.tensor_copy(xs[:, 64:128], ps[:, 0:64]), "shifted_rows")
            m2 = dve.do(lambda e: e.tensor_copy(xs[:, 0:64], x[:, i, 0:64]), "shifted_rows")
            r_small.done(ps_n, m1)
            s["xs"] = (n, xs, norm_factors(xs[:, :], m2))

        def ff_norm(s):
            n, xs, factors = s["xs"]
            xn_n, xn, m = layer_norm(xs[:, :], factors)
            r_xs.done(n, m)
            s["xn"] = (xn_n, xn, m)

        def ff_turn(s):
            xn_n, xn, m = s["xn"]
            layer, g, k = s["layer"], s["group"], s["tile"] % GROUP
            ps_n, ps, free = r_small.take()
            pe.wait(m, free)
            m = pe.do(lambda e: e.transpose(ps[:, 0:P], xn[:, :], ident), "tile_turned")
            r_xn.done(xn_n, m)
            if k == 0:
                g["fx_n"], g["fx"], g["fx_free"] = r_ffx.take()
            act.wait(m, g["fx_free"], m_param)
            fx = g["fx"]
            g["fx_m"] = act.do(lambda e: e.activation(
                fx[:, k * P:(k + 1) * P], ps[:, 0:P], ACT.Identity, bias=cols[:, B_LNB + layer:B_LNB + layer + 1],
                scale=cols[:, B_LNG + layer:B_LNG + layer + 1]), "tile_copied")
            r_small.done(ps_n, g["fx_m"])

        def ff_hidden(s):
            if s["tile"] % GROUP != GROUP - 1:
                return
            layer, g = s["layer"], s["group"]
            b = layer % 2
            g["h_n"], hid, h_free = r_hid.take()
            g["h"] = hid
            for c in range(FF_CHUNKS):
                ps_n, ps, free = r_big.take()
                pe.wait(free, g["fx_m"], layer_loaded[layer])
                pe.do(lambda e, c=c, ps=ps: e.matmul(ps[:, 0:512], w_ff1[b][:, FF_CHUNKS + c, :], g["fx"][:, :],
                                                     start=True, stop=True))
                m = pe.do(lambda e, c=c, ps=ps: e.matmul(ps[:, 512:1024], w_ff1[b][:, c, :], g["fx"][:, :],
                                                         start=True, stop=True), "hidden_projected")
                at = B_FF1 + 2 * FF_CHUNKS * layer + c
                g_n, gate, g_free = r_gate.take()
                act.wait(m, g_free)
                m_g = act.do(lambda e, ps=ps, at=at, gate=gate: e.activation(
                    gate[:, :], ps[:, 0:512], ACT.Gelu,
                    bias=cols[:, at + FF_CHUNKS:at + FF_CHUNKS + 1]), "gated")
                dve.wait(m_g, h_free)
                g["h_m"] = dve.do(lambda e, ps=ps, at=at, gate=gate, c=c: e.scalar_tensor_tensor(
                    out=hid[:, c, :], in0=ps[:, 512:1024], scalar=cols[:, at:at + 1], in1=gate[:, :],
                    op0=ALU.add, op1=ALU.mult), "hidden_ready")
                r_gate.done(g_n, g["h_m"])
                r_big.done(ps_n, g["h_m"])
            exp_tables()
            r_ffx.done(g["fx_n"], m)

        def ff_output(s):
            layer, i, g = s["layer"], s["tile"], s["group"]
            k, hid = i % GROUP, g["h"]
            ps_n, ps, free = r_small.take()
            pe.wait(free, g["h_m"])
            at = R_FF2 + layer * D
            pe.do(lambda e: e.matmul(ps[:, 0:D], ones_row, rows[:, at:at + D], start=True, stop=False))
            for c in range(FF_CHUNKS):
                m = pe.do(lambda e, c=c: e.matmul(ps[:, 0:D], hid[:, c, k * P:(k + 1) * P], w_ff2[layer % 2][:, c, :],
                                                  start=False, stop=(c == FF_CHUNKS - 1)),
                          "ff_projected" if c == FF_CHUNKS - 1 else None)
            dve.wait(m, x_read[i])
            x_ready[i] = dve.do(lambda e: e.tensor_tensor(x[:, i, :], x[:, i, :], ps[:, 0:D], ALU.add), "x_updated")
            r_small.done(ps_n, x_ready[i])
            if k == GROUP - 1:
                r_hid.done(g["h_n"], m)
            if i == TILES - 1 and layer + 2 < DEPTH:
                layer_free[layer % 2] = [m]
                load_layer(layer + 2)
            if layer == DEPTH - 1:
                pool.wait(x_ready[i])
                m = pool.do(lambda e: e.tensor_tensor(x_in[:, i, :], x_in[:, i, :], x[:, i, :], ALU.add),
                            "result_ready")
                sp.wait(m)
                s["stored"] = sp.do(lambda e: e.dma_start(out[i * P:(i + 1) * P, :], x_in[:, i, :]), "stored", 16)

        r_xs = ring("xs", 2, [P, D])

        logits = sb("logits", [P, TILES, EXPERTS])
        onehot = sb("onehot", [P, TILES, EXPERTS])
        onehot_b = sb("onehot_b", [P, TILES, EXPERTS], BF16)
        top = sb("top", [P, 8, TILES])
        slot = sb("slot", [P, 2, TILES], I32)
        r_b2 = ring("moe_b2", 4, [1, D])
        r_row = ring("moe_row", 2, [P, D])
        zeros_n, zeros_buf, _ = r_hid.take()
        zeros = zeros_buf[:, 0:2, :].rearrange("p a b -> p (a b)")
        dispatched = t["dispatched"]
        answers = t["answers"]

        m_z = pool.do(lambda e: e.memset(zeros, 0.0), "zeros")
        sp.wait(m_z)
        d_v = dispatched.rearrange("(h p s) d -> h p (s d)", h=2, p=P)
        for h in range(2):
            m_clear = sp.do(lambda e, h=h: e.dma_start(d_v[h], zeros), "dispatch_cleared", 16)
        m_zero_row = sp.do(lambda e: e.dma_start(answers[SLOTS:SLOTS + 1, :], zeros_buf[0:1, 0, 0:D]), "zero_row", 16)
        r_hid.done(zeros_n, m_clear, m_zero_row)

        expert_w = {}

        def load_expert(e_id):
            n1, both, free1 = r_cos.take()
            n2, b2, free2 = r_b2.take()
            w1, w2 = both[:, 0:HIDDEN], both[:, HIDDEN:].rearrange("p (c d) -> p c d", d=D)
            sp.wait(free1, free2)
            sem = f"expert_weights{n1}"
            sp.do(lambda e: e.dma_start(w1, t["mw1"][e_id]), sem, 16)
            sp.do(lambda e: e.dma_start(b2[:, :], t["mb2"][e_id:e_id + 1, :]), sem, 16)
            m = sp.do(lambda e: e.dma_start(w2, t["mw2"][e_id].rearrange("(c p) d -> p c d", p=P)), sem, 16)
            expert_w[e_id] = (n1, w1, w2, n2, b2, m)

        for e_id in range(4):
            load_expert(e_id)

        raw_logits = sb("raw_logits", [P, TILES, EXPERTS])

        def route_norm(s):
            i = s["tile"]
            s["kept"] = layer_norm(x[:, i, :], norm_factors(x[:, i, :], x_ready[i]), place=x_in[:, i, :])[2]

        def route_logits(s):
            i = s["tile"]
            xt_n, xt, m_t, _ = transposed(x_in[:, i, :], s["kept"])
            ps_n, ps, free = r_small.take()
            pe.wait(m_t, free, m_param)
            pe.do(lambda e: e.matmul(ps[:, 0:EXPERTS], xt[:, :], wg[:, :], start=True, stop=False))
            m = pe.do(lambda e: e.matmul(ps[:, 0:EXPERTS], ones_row, rows[:, R_BG:R_BG + EXPERTS],
                                         start=False, stop=True), "logits_ready")
            r_xt.done(xt_n, m)
            dve.wait(m)
            s["logits"] = dve.do(lambda e: e.tensor_copy(raw_logits[:, i, :], ps[:, 0:EXPERTS]), "logits_copied")
            r_small.done(ps_n, s["logits"])

        def routed(tiles):
            lgv = raw_logits[:, :, :]
            m_l = [s["logits"] for s in tiles]
            kept = [s["kept"] for s in tiles]

            def chain(fn, *marks):
                dve.wait(*marks)
                m = dve.do(fn, "routing")
                dve.wait(m)
                return m

            whole = [P, TILES, EXPERTS]
            spread = lambda n: top[:, n, :, None].to_broadcast(whole)
            expert = const[:, C_EXPERT:C_EXPERT + EXPERTS]
            experts = expert[:, None, :].to_broadcast(whole)
            chain(lambda e: e.tensor_reduce(top[:, 0, :], lgv, AX_X, ALU.max), m_l)
            m = chain(lambda e: e.tensor_tensor(logits[:, :, :], lgv, spread(0), ALU.subtract))
            act.wait(m)
            m_e = act.do(lambda e: e.activation(onehot[:, :, :], logits[:, :, :], ACT.Exp), "gate_exponentials")
            chain(lambda e: e.tensor_reduce(top[:, 1, :], onehot[:, :, :], AX_X, ALU.add), m_e)
            chain(lambda e: e.reciprocal(top[:, 2, :], top[:, 1, :]))
            chain(lambda e: e.tensor_scalar(logits[:, :, :], logits[:, :, :], 0.0, -64.0, ALU.is_ge, ALU.mult))
            chain(lambda e: e.tensor_tensor(logits[:, :, :], logits[:, :, :], experts, ALU.add))
            chain(lambda e: e.tensor_reduce(top[:, 3, :], logits[:, :, :], AX_X, ALU.min))
            chain(lambda e: e.tensor_scalar(top[:, 3, :], top[:, 3, :], 64.0, None, ALU.add))
            chain(lambda e: e.tensor_tensor(onehot[:, :, :], experts, spread(3), ALU.is_equal))
            m = chain(lambda e: e.tensor_copy(onehot_b[:, :, :], onehot[:, :, :]))
            ps_n, ps, free = r_small.take()
            pv = ps[:, 0:TILES * EXPERTS].rearrange("p (t e) -> p t e", e=EXPERTS)
            pe.wait(m, free, m_bf)
            pe.do(lambda e: e.matmul(pv, tri_b[:, :], onehot_b[:, :, :], start=True, stop=True))
            for i in range(TILES - 1):
                rest = TILES - 1 - i
                m = pe.do(lambda e, i=i, rest=rest: e.matmul(
                    pv[:, i + 1:, :], ones_b[:, :], onehot_b[:, i:i + 1, :].to_broadcast([P, rest, EXPERTS]),
                    start=False, stop=True, skip_group_check=True), "earlier_counted" if rest == 1 else None)
            chain(lambda e: e.tensor_tensor(logits[:, :, :], pv, onehot[:, :, :], ALU.mult), m)
            m = chain(lambda e: e.tensor_reduce(top[:, 4, :], logits[:, :, :], AX_X, ALU.add))
            r_small.done(ps_n, m)
            chain(lambda e: e.tensor_scalar(top[:, 5, :], top[:, 3, :], float(CAP), None, ALU.mult))
            chain(lambda e: e.tensor_tensor(top[:, 5, :], top[:, 5, :], top[:, 4, :], ALU.add))
            chain(lambda e: e.tensor_scalar(top[:, 6, :], top[:, 4, :], float(CAP), float(2 * SLOTS),
                                            ALU.is_ge, ALU.mult))
            chain(lambda e: e.tensor_tensor(top[:, 5, :], top[:, 5, :], top[:, 6, :], ALU.add))
            chain(lambda e: e.tensor_copy(slot[:, 0, :], top[:, 5, :]))
            chain(lambda e: e.tensor_scalar(top[:, 7, :], top[:, 5, :], float(SLOTS), None, ALU.min))
            m = chain(lambda e: e.tensor_copy(slot[:, 1, :], top[:, 7, :]))
            pool.wait(m, m_clear)
            for i in range(TILES):
                pool.wait(kept[i])
                m_disp = pool.do(lambda e, i=i: e.indirect_dma_start(
                    out=dispatched, out_offset=bass.IndirectOffsetOnAxis(ap=slot[:, 0, i:i + 1], axis=0),
                    in_=x_in[:, i, :], in_offset=None, bounds_check=SLOTS - 1, oob_is_err=False), "dispatched", 16)
            m_ans = []
            sp.wait(m_disp)
            rows_in = {}

            def load_rows(e_id):
                n, xr, free = r_row.take()
                sp.wait(free)
                rows_in[e_id] = (n, xr, sp.do(lambda e: e.dma_start(xr[:, :], dispatched[e_id * CAP:(e_id + 1) * CAP, :]),
                                              f"slots_loaded{n}", 16))

            load_rows(0)
            for x_id in range(EXPERTS):
                if x_id + 1 < EXPERTS:
                    load_rows(x_id + 1)
                n, xr, m = rows_in[x_id]
                n1, w1, w2, n2, b2, m_w = expert_w[x_id]
                xt_n, xt, m_t, m_read = transposed(xr[:, :], m)
                r_row.done(n, m_read)
                ps_n, ps, free = r_big.take()
                pe.wait(free, m_t, m_w)
                for c in range(HIDDEN // P):
                    m = pe.do(lambda e, c=c, ps=ps, w1=w1, xt=xt: e.matmul(
                        ps[:, c * P:(c + 1) * P], w1[:, c * P:(c + 1) * P], xt[:, :], start=True, stop=True),
                        "expert_hidden" if c == HIDDEN // P - 1 else None)
                r_xt.done(xt_n, m)
                h_n, hb, h_free = r_sq.take()
                act.wait(m, h_free)
                for c in range(HIDDEN // P):
                    at = B_MOE1 + x_id * (HIDDEN // P) + c
                    m = act.do(lambda e, c=c, ps=ps, hb=hb, at=at: e.activation(
                        hb[:, c * P:(c + 1) * P], ps[:, c * P:(c + 1) * P], ACT.Relu, bias=cols[:, at:at + 1]),
                        "expert_relu")
                r_big.done(ps_n, m)
                ps_n, ps, free = r_small.take()
                pe.wait(free, m)
                pe.do(lambda e, ps=ps, b2=b2: e.matmul(ps[:, 0:D], ones_row, b2[:, :],
                                                       start=True, stop=False))
                for c in range(HIDDEN // P):
                    m = pe.do(lambda e, c=c, ps=ps, hb=hb, w2=w2: e.matmul(
                        ps[:, 0:D], hb[:, c * P:(c + 1) * P], w2[:, c, :], start=False, stop=(c == HIDDEN // P - 1)),
                        "expert_output" if c == HIDDEN // P - 1 else None)
                r_b2.done(n2, m)
                r_cos.done(n1, m)
                r_sq.done(h_n, m)
                y_n, y, y_free = r_xn.take()
                dve.wait(m, y_free)
                m = dve.do(lambda e, y=y, ps=ps: e.tensor_copy(y[:, :], ps[:, 0:D]), "answer_copied")
                r_small.done(ps_n, m)
                act.wait(m)
                m = act.do(lambda e, x_id=x_id, y=y: e.dma_start(answers[x_id * CAP:(x_id + 1) * CAP, :], y[:, :]),
                           f"answer_stored{y_n}", 16)
                r_xn.done(y_n, m)
                m_ans.append(m)
                if x_id + 4 < EXPERTS:
                    load_expert(x_id + 4)
            answered.extend(m_ans[-len(r_xn.buffers):])

        answered = []

        def fetch_answer(s):
            i = s["tile"]
            n, y, free = r_back.take()
            pool.wait(free, answered, m_zero_row)
            m = pool.do(lambda e: e.indirect_dma_start(
                out=y[:, :], out_offset=None, in_=answers,
                in_offset=bass.IndirectOffsetOnAxis(ap=slot[:, 1, i:i + 1], axis=0),
                bounds_check=SLOTS, oob_is_err=False), f"answer_fetched{n}", 16)
            s["back"] = (n, y, m)

        def add_answer(s):
            i = s["tile"]
            n, y, m = s["back"]
            dve.wait(m)
            x_ready[i] = dve.do(lambda e: e.scalar_tensor_tensor(
                out=x[:, i, :], in0=y[:, :], scalar=top[:, 2, i:i + 1], in1=x[:, i, :],
                op0=ALU.mult, op1=ALU.add), "x_updated")
            r_back.done(n, x_ready[i])

        r_back = ring("back", 4, [P, D])

        def run(stages):
            for step in range(max(len(items) + lag for _, items, lag in stages)):
                for stage, items, lag in stages:
                    if 0 <= step - lag < len(items):
                        stage(items[step - lag])

        project = lambda which: lambda s: (project_layer if s["kind"] == "L" else project_cross)(s, which)
        turn_of = lambda which: lambda s: turn(s, which)

        first = [{"kind": "A", "tile": i} for i in range(TILES)]
        run([
            (scores, first, 2),
            (turn_probabilities, first, 3),
            (input_cross, first, 0),
            (project("k"), first, 1),
            (exponentials, first, 2),
            (weigh, first, 3),
            (project("q"), first, 1),
            (normalize, first, 2),
            (route_norm, first, 4),
            (output, first, 3),
            (project_cross_v, first, 1),
            (route_logits, first, 4),
        ])
        routed(first)
        layer_free[1] = [first[-1]["done"]]
        load_layer(1)

        second = [{"kind": "X", "tile": i} for i in range(TILES)]
        groups = [[{} for _ in range(TILES // GROUP)] for _ in range(DEPTH)]
        layers = [{"kind": "L", "layer": n, "tile": i, "group": groups[n][i // GROUP]}
                  for n in range(DEPTH) for i in range(TILES)]
        start = 8
        of = lambda stage, which: lambda s: stage(s, which)
        run([
            (fetch_answer, second, 0),
            (add_answer, second, 2),
            (input_cross, second, 3),
            (scores, layers, start + 2),
            (turn_probabilities, layers, start + 3),
            (scores, second, 5),
            (project("q"), layers, start),
            (ff_input, layers, start + 4),
            (exponentials, layers, start + 2),
            (exponentials, second, 5),
            (of(rotate, "q"), layers, start),
            (turn_probabilities, second, 6),
            (project("k"), layers, start),
            (normalize, layers, start + 2),
            (normalize, second, 5),
            (of(rotate, "k"), layers, start),
            (ff_norm, layers, start + 4),
            (of(square, "q"), layers, start),
            (weigh, layers, start + 3),
            (ff_hidden, layers, start + 5),
            (project_cross_v, second, 4),
            (project("q"), second, 4),
            (project("k"), second, 4),
            (project("v"), layers, start),
            (of(square, "k"), layers, start),
            (of(sum_squares, "q"), layers, start),
            (turn_of("q"), layers, start + 1),
            (turn_of("k"), layers, start + 1),
            (weigh, second, 6),
            (of(sum_squares, "k"), layers, start),
            (inverse_norms, layers, start),
            (of(scale_rows, "q"), layers, start),
            (of(scale_rows, "k"), layers, start),
            (ff_output, layers, start + 8),
            (ff_turn, layers, start + 4),
            (output, layers, start + 3),
            (output, second, 6),
            (input_layer, layers, start - 1),
        ])
        sp.wait(layers[-1]["stored"])

        sems = {name: ctx.enter_context(nc.semaphore(name)) for name in counts}
        block = ctx.enter_context(nc.Block())

        @block.sync
        def _(e):
            sp.play(e, sems)

        @block.scalar
        def _(e):
            act.play(e, sems)

        @block.gpsimd
        def _(e):
            pool.play(e, sems)

        @block.vector
        def _(e):
            dve.play(e, sems)

        @block.tensor
        def _(e):
            pe.play(e, sems)


def shape_constants():
    f = np.float32
    c = np.zeros((P, C_END), f)
    tok = np.arange(P)
    c[:, C_IDENT:C_IDENT + P] = np.eye(P)
    c[:, C_SHIFT:C_SHIFT + P] = (tok[:, None] + 1 == tok[None, :]) & (tok[None, :] % SEQ != 0)
    c[:, C_TRI:C_TRI + P] = tok[:, None] < tok[None, :]
    c[:, C_ONES:C_ONES + P] = 1.0
    q, k = (tok % SEQ)[:, None], (np.arange(512) % SEQ)[None, :]
    c[:, C_MASK:C_MASK + 512] = np.where((k <= q) & (q <= k + WINDOW), 0.0, MASKED)
    half = np.arange(0, HEAD_D, 2, dtype=f)
    inv_freq = (f(1.0) / (f(10000.0) ** (half / f(HEAD_D)))).astype(f)
    pos = np.arange(SEQ, dtype=f)
    freqs = (pos[:, None] * inv_freq[None, :]).astype(f)
    base = ((half + f(0.4 * HEAD_D)) / f(1.4 * HEAD_D)).astype(f)
    power = ((pos - f(SEQ // 2)) / f(WINDOW // 2)).astype(f)
    scale = (base[None, :] ** power[:, None]).astype(f)
    cos, sin = np.cos(freqs).astype(f), np.sin(freqs).astype(f)
    for s, sc in enumerate((scale, f(1.0) / scale)):
        block = np.concatenate([cos * sc, cos * sc, -sin * sc, sin * sc], 1)
        c[:, C_ROPE + 2 * s * HEAD_D:C_ROPE + 2 * (s + 1) * HEAD_D] = np.tile(block, (2, 1))
    c[:, C_EXPERT:C_EXPERT + EXPERTS] = np.arange(EXPERTS)
    return c


def kernel(**inputs):
    import concourse.bacc as bacc
    from concourse.bass_utils import run_bass_kernel_spmd

    v = {k: np.ascontiguousarray(a) for k, a in inputs.items()}
    chunks = 2 * FF_CHUNKS
    ff1 = np.zeros((DEPTH, D, 2, FF_CHUNKS * P), np.float32)
    ff1[:, :, :, :FF] = v["L1_ffn_W1"].reshape(DEPTH, D, 2, FF)
    ffb = np.zeros((DEPTH, 2, FF_CHUNKS * P), np.float32)
    ffb[:, :, :FF] = v["L1_ffn_b1"].reshape(DEPTH, 2, FF)
    ff2 = np.zeros((DEPTH, FF_CHUNKS * P, D), np.float32)
    ff2[:, :FF] = v["L1_ffn_W2"]
    cols = np.concatenate([
        v["L0_ffn_b1"].reshape(EXPERTS * HIDDEN // P, P).T,
        ffb.reshape(DEPTH * chunks, P).T, v["L1_ffn_ln_g"].T, v["L1_ffn_ln_b"].T], 1)
    rows = np.concatenate([v["L0_xattn_bo"], v["L0_ffn_bg"], v["L1_xattn_bo"],
                           v["L1_ffn_b2"].reshape(-1)])[None]
    wx = np.zeros((P, 4, D), np.float32)
    for n, name in enumerate(("Wq", "Wk", "Wv", "Wo")):
        w = v["L1_xattn_" + name].T
        wx[:w.shape[0], n] = w
    arrays = {
        "const": shape_constants(),
        "x": v["x"].reshape(-1, D),
        "ctx_t": np.ascontiguousarray(v["ctx_768"].reshape(-1, CTX_D).T),
        "wq": v["L0_xattn_Wq"], "wk": v["L0_xattn_Wk"], "wv": v["L0_xattn_Wv"], "wo": v["L0_xattn_Wo"],
        "cols": np.ascontiguousarray(cols), "rows": np.ascontiguousarray(rows), "wx": wx,
        "wg": v["L0_ffn_Wg"],
        "scales": np.stack([v["L1_ffn_q_scale"], v["L1_ffn_k_scale"]])[None],
        "wqkv": v["L1_ffn_Wqkv"], "lwo": v["L1_ffn_Wo"],
        "ff1": ff1.reshape(DEPTH, D, chunks, P), "ff2": ff2,
        "mw1": v["L0_ffn_W1"], "mw2": v["L0_ffn_W2"], "mb2": v["L0_ffn_b2"],
    }
    nc = bacc.Bacc("TRN2", target_bir_lowering=False, num_devices=1)
    t = {name: nc.dram_tensor(name + "_dram", a.shape, mybir.dt.from_np(a.dtype), kind="ExternalInput").ap()
         for name, a in arrays.items()}
    t["dispatched"] = nc.dram_tensor("dispatched", [SLOTS, D], F32, kind="Internal").ap()
    t["answers"] = nc.dram_tensor("answers", [SLOTS + 1, D], F32, kind="Internal").ap()
    out = nc.dram_tensor("out_dram", [BATCH * SEQ, D], F32, kind="ExternalOutput").ap()
    build(nc, t, out)
    r = run_bass_kernel_spmd(nc, [{name + "_dram": a for name, a in arrays.items()}], core_ids=[0])
    return r.results[0]["out_dram"].reshape(BATCH, SEQ, D)
```

```python
from contextlib import ExitStack

import numpy as np

import concourse.bass as bass
from concourse import mybir

F32 = mybir.dt.float32
BF16 = mybir.dt.bfloat16
I32 = mybir.dt.int32
ALU = mybir.AluOpType
ACT = mybir.ActivationFunctionType
AX_X = mybir.AxisListType.X

P = 128
D = 128
BATCH, SEQ = 32, 64
TILES = BATCH * SEQ // P
CTX_D = 96
HEADS, HEAD_D = 16, 64
INNER = HEADS * HEAD_D
PAIRS = HEADS // 2
XHEADS, XHEAD_D = 4, 32
EXPERTS, HIDDEN = 16, 512
CAP = BATCH * SEQ // EXPERTS
SLOTS = EXPERTS * CAP
DEPTH = 6
WINDOW = 32
FF = D * 4 * 2 // 3
FF_CHUNKS = 3
GROUP = 4
LN_EPS = 1e-5
NORM_FLOOR = 1e-24
LN_SHIFT = 17
MASKED = -1e30

C_IDENT, C_SHIFT, C_TRI, C_ONES, C_MASK = 0, 128, 256, 384, 512
C_ROPE, C_EXPERT, C_END = 576, 832, 848
B_MOE1, B_FF1, B_LNG, B_LNB, B_END = 0, 64, 100, 106, 112
R_BO0, R_BG, R_BO1, R_END = 0, 128, 144, 272


class Mark:

    def __init__(self, sem, value):
        self.sem, self.value = sem, value


class Queue:

    def __init__(self, counts):
        self.steps, self.waited, self.counts = [], {}, counts

    def wait(self, *marks):
        for m in marks:
            if isinstance(m, (list, tuple)):
                self.wait(*m)
            elif m is not None and self.waited.get(m.sem, 0) < m.value:
                self.waited[m.sem] = m.value
                self.steps.append((None, m.sem, m.value))

    def do(self, instruction, sem=None, by=1):
        self.steps.append((instruction, sem, by))
        if sem is None:
            return None
        self.counts[sem] = self.counts.get(sem, 0) + by
        return Mark(sem, self.counts[sem])

    def play(self, engine, sems):
        for instruction, sem, value in self.steps:
            if instruction is None:
                engine.wait_ge(sems[sem], value)
            elif sem is None:
                instruction(engine)
            else:
                instruction(engine).then_inc(sems[sem], value)


class Ring:

    def __init__(self, buffers):
        self.buffers, self.free, self.turn = buffers, [[] for _ in buffers], -1

    def take(self):
        self.turn = (self.turn + 1) % len(self.buffers)
        free, self.free[self.turn] = self.free[self.turn], None
        assert free is not None, "a buffer is taken before its last use is written down"
        return self.turn, self.buffers[self.turn], free

    def done(self, n, *marks):
        self.free[n] = list(marks)


def build(nc, t, out):
    counts = {}
    pe, act, dve, pool, sp = (Queue(counts) for _ in range(5))
    ctx = ExitStack()
    with ctx:
        def sb(name, shape, dt=F32):
            return ctx.enter_context(nc.sbuf_tensor(name, shape, dt))

        x = sb("x", [P, TILES, D])
        x_in = sb("x_in", [P, TILES, D])
        ctx_t = sb("ctx_t", [CTX_D, BATCH * SEQ])
        const = sb("const", [P, C_END])
        cols = sb("cols", [P, B_END])
        rows = sb("rows", [1, R_END])
        scales = sb("scales", [P, 2, DEPTH, HEAD_D])
        rope = sb("rope", [P, DEPTH, 4, HEAD_D])
        ff_bias = sb("ff_bias", [P, DEPTH, D])
        tri_b = sb("tri_b", [P, P], BF16)
        ones_b = sb("ones_b", [P, P], BF16)
        w_in = [sb(f"w_in{n}", [P, 3 * INNER]) for n in range(2)]
        w_out = [sb(f"w_out{n}", [P, PAIRS, D]) for n in range(2)]
        w_ff1 = [sb(f"w_ff1{n}", [P, 2 * FF_CHUNKS, P]) for n in range(2)]
        w_ff2 = [sb(f"w_ff2{n}", [P, FF_CHUNKS, D]) for n in range(2)]
        wx = sb("wx", [P, 4, D])
        wg = sb("wg", [D, EXPERTS])

        def ring(name, n, shape, dt=F32):
            return Ring([sb(f"{name}{i}", shape, dt) for i in range(n)])

        r_stat = ring("stat", 8, [P, 12])
        r_xn = ring("xn", 4, [P, D])
        r_xt = ring("xt", 5, [P, P])
        r_raw = ring("raw", 2, [P, INNER])
        r_sq = ring("sq", 2, [P, INNER])
        r_cos = ring("cos", 4, [P, INNER])
        r_sin = ring("sin", 2, [P, INNER])
        r_norm = ring("norm", 2, [P, 3, 2, HEADS])
        wide_rings = {
            "q": ring("qt", 1, [P, PAIRS, P]), "k": ring("kt", 1, [P, PAIRS, P]), "v": ring("v", 4, [P, INNER]),
            "p": ring("p", 2, [P, INNER]), "pt": ring("pt", 1, [P, INNER]), "ot": ring("ot", 1, [P, PAIRS, P])}
        narrow_rings = {
            "q": ring("xqt", 2, [P, 1, P]),
            "p": ring("xp", 2, [P, 2 * P]), "pt": ring("xpt", 1, [P, 2 * P]), "ot": ring("xot", 1, [P, 1, P])}
        rings_of = {"A": wide_rings, "L": wide_rings, "X": narrow_rings}
        xk_all = sb("xk_all", [P, 1, BATCH * SEQ])
        xv_all = sb("xv_all", [P, TILES * D])
        r_soft = ring("soft", 5, [P, 3 * HEADS])
        r_ffx = ring("ffx", 1, [P, GROUP * P])
        r_gate = ring("gate", 2, [P, GROUP * P])
        r_hid = ring("hid", 1, [P, FF_CHUNKS, GROUP * P])
        r_big = Ring([ctx.enter_context(nc.psum_tensor(f"big{i}", [P, 1024], F32)) for i in range(3)])
        r_small = Ring([ctx.enter_context(nc.psum_tensor(f"small{i}", [P, 512], F32)) for i in range(2)])

        ident = const[:, C_IDENT:C_IDENT + P]
        shift = const[:, C_SHIFT:C_SHIFT + P]
        ones_row = const[0:1, C_ONES:C_ONES + P]

        x_d = t["x"].rearrange("(t p) d -> p t d", p=P)
        x_loaded = []

        def load_x(q):
            a, b = q * TILES // 4, (q + 1) * TILES // 4
            m = sp.do(lambda e: e.dma_start(x[:, a:b, :], x_d[:, a:b, :]), f"x_loaded{q}", 16)
            x_loaded.extend((b - a) * [m])

        def load_first(queue, n, name):
            k = D if n == 0 else CTX_D
            return queue.do(lambda e: e.dma_start(w_in[1][0:k, n * INNER:(n + 1) * INNER], t[name]),
                            f"first_{name}_loaded", 16)

        m_wk = load_first(act, 1, "wk")
        m_ctx = act.do(lambda e: e.dma_start(ctx_t[:, :], t["ctx_t"]), "context_loaded", 16)
        load_x(0)
        m_const = sp.do(lambda e: e.dma_start(const[:, :], t["const"]), "const_loaded", 16)
        m_wq = load_first(sp, 0, "wq")
        m_wv = load_first(sp, 2, "wv")
        load_x(1)
        m_wo = sp.do(lambda e: e.dma_start(
            w_out[1][:, :, :], t["wo"].rearrange("(j p) n -> p j n", p=P)), "first_wo_loaded", 16)
        for dst, src in ((cols[:, :], t["cols"]), (rows[:, :], t["rows"]), (wx[:, :, :], t["wx"]),
                         (wg[:, :], t["wg"]), (scales[:, :, :, :], t["scales"].to_broadcast([P, 2, DEPTH, HEAD_D])),
                         (ff_bias[:, :, :], t["ff_bias"].to_broadcast([P, DEPTH, D]))):
            m_param = sp.do(lambda e, dst=dst, src=src: e.dma_start(dst, src), "parameters_loaded", 16)
        load_x(2)
        load_x(3)

        layer_free = [[], []]
        layer_loaded = {}

        def load_layer(n):
            b = n % 2
            sp.wait(layer_free[b])
            sem = f"layer_weights{b}"
            sp.do(lambda e: e.dma_start(w_in[b][:, :], t["wqkv"][n]), sem, 16)
            sp.do(lambda e: e.dma_start(w_out[b][:, :, :], t["lwo"][n].rearrange("(j p) n -> p j n", p=P)), sem, 16)
            sp.do(lambda e: e.dma_start(w_ff1[b][:, :, :], t["ff1"][n]), sem, 16)
            layer_loaded[n] = sp.do(lambda e: e.dma_start(
                w_ff2[b][:, :, :], t["ff2"][n].rearrange("(c p) n -> p c n", p=P)), sem, 16)

        load_layer(0)

        dve.wait(m_const)
        for dst, at, n in ((tri_b, C_TRI, P), (ones_b, C_ONES, P)):
            m_bf = dve.do(lambda e, dst=dst, at=at, n=n: e.tensor_copy(dst[:, :], const[:, at:at + n]), "bf16_constants")
        pool.wait(m_const, m_param)
        for n in range(DEPTH):
            for s in range(2):
                base = const[:, C_ROPE + 2 * s * HEAD_D:C_ROPE + 2 * (s + 1) * HEAD_D]
                m_rope = pool.do(lambda e, n=n, s=s, base=base: e.tensor_tensor(
                    rope[:, n, 2 * s, :], base[:, 0:HEAD_D], scales[:, s, n, :], ALU.mult), "rope_tables")
                half = HEAD_D // 2
                for h in range(2):
                    m_rope = pool.do(lambda e, n=n, s=s, base=base, h=h: e.tensor_tensor(
                        rope[:, n, 2 * s + 1, h * half:(h + 1) * half],
                        base[:, HEAD_D + h * half:HEAD_D + (h + 1) * half],
                        scales[:, s, n, (1 - h) * half:(2 - h) * half], ALU.mult), "rope_tables")

        x_ready = list(x_loaded)
        x_read = [[] for _ in range(TILES)]

        exp_tables = lambda: act.do(lambda e: e.preload_act_table_set("natural_log_exp_and_others"))
        exp_tables()

        def norm_factors(src, mark):
            sn, st, sfree = r_stat.take()
            dve.wait(mark, sfree)
            m = dve.do(lambda e: e.bn_stats(st[:, 0:6], src), "norm_stats")
            dve.wait(m)
            m = dve.do(lambda e: e.bn_aggr(st[:, 6:8], st[:, 0:6]), "norm_stats")
            act.wait(m)
            m = act.do(lambda e: e.activation(st[:, 8:9], st[:, 7:8], ACT.Ln, bias=st[:, 9:10]), "log")
            act.wait(m)
            m = act.do(lambda e: e.activation(st[:, 8:9], st[:, 8:9], ACT.Exp, scale=-0.5), "inverse_root")
            return sn, st, m

        def layer_norm(src, factors, place=None):
            sn, st, m = factors
            n, xn, free = r_xn.take() if place is None else (None, None, None)
            dve.wait(m, free)
            dst = xn[:, :] if place is None else place
            m = dve.do(lambda e: e.tensor_scalar(dst, src, st[:, 6:7], st[:, 8:9], ALU.subtract, ALU.mult),
                       "normalized")
            r_stat.done(sn, m)
            return n, xn, m

        for st in r_stat.buffers:
            m_eps = dve.do(lambda e, st=st: e.memset(st[:, 9:10], LN_EPS), "constants_set")
        act.wait(m_eps)
        floor_shift = sb("floor_shift", [P, 1])
        m_fs = dve.do(lambda e: e.memset(floor_shift[:, :], 0.5 * LN_SHIFT * float(np.log(2.0))), "constants_set")
        act.wait(m_fs)

        def transposed(src, mark):
            ps_n, ps, ps_free = r_small.take()
            pe.wait(mark, ps_free, m_const)
            m_read = pe.do(lambda e: e.transpose(ps[:, 0:P], src, ident), "tile_turned")
            n, xt, free = r_xt.take()
            act.wait(m_read, free)
            m = act.do(lambda e: e.activation(xt[:, :], ps[:, 0:P], ACT.Copy), "tile_copied")
            r_small.done(ps_n, m)
            return n, xt, m, m_read

        def evacuate(ps_n, ps, width, ring_to, mark, sem):
            n, dst, free = ring_to.take()
            flat = dst[:, :] if len(dst.shape) == 2 else dst[:, :, :].rearrange("p a b -> p (a b)")
            act.wait(mark, free)
            m = act.do(lambda e: e.activation(flat[:, 0:width], ps[:, 0:width], ACT.Copy), sem)
            r_big.done(ps_n, m)
            return n, dst, m

        def input_factors(s):
            i = s["tile"]
            s["factors"] = norm_factors(x[:, i, :], x_ready[i])

        def input_norm(s):
            s["xn"] = layer_norm(x[:, s["tile"], :], s["factors"])

        def input_turn(s):
            n, xn, m = s["xn"]
            s["xt_n"], s["xt"], s["xt_m"], m_read = transposed(xn[:, :], m)
            r_xn.done(n, m_read)

        def input_layer(s):
            i = s["tile"]
            ps_n, ps, ps_free = r_small.take()
            pe.wait(x_ready[i], ps_free)
            pe.do(lambda e: e.matmul(ps[0:64, 0:P], x[:, i, 0:64], ident, start=True, stop=True))
            m = pe.do(lambda e: e.matmul(ps[64:128, 0:P], x[:, i, 64:128], shift, start=True, stop=True),
                      "shifted")
            x_read[i] = [m]
            n, xt, free = r_xt.take()
            act.wait(m, free)
            m = act.do(lambda e: e.activation(xt[:, :], ps[:, 0:P], ACT.Copy), "tile_copied")
            r_small.done(ps_n, m)
            s["xt_n"], s["xt"], s["xt_m"] = n, xt, m

        def project_cross(s, which):
            i, first = s["tile"], s["kind"] == "A"
            n_out = PAIRS if first else 1
            ps_n, ps, free = r_big.take()
            if which == "q":
                rhs, k, off = s["xt"][:, :], D, 0
                pe.wait(free, s["xt_m"], m_wq if first else m_param)
            else:
                rhs, k, off = ctx_t[:, i * P:(i + 1) * P], CTX_D, INNER
                pe.wait(free, m_ctx, m_wk)
            for j in range(n_out):
                lhs = w_in[1][0:k, off + j * P:off + (j + 1) * P] if first else wx[:, 0, :]
                m = pe.do(lambda e, j=j, lhs=lhs: e.matmul(ps[:, j * P:(j + 1) * P], lhs, rhs, start=True, stop=True),
                          "cross_projected" if j == n_out - 1 else None)
            if which == "q":
                r_xt.done(s["xt_n"], m)
            s[which + "_n"], s[which], s[which + "_m"] = evacuate(
                ps_n, ps, n_out * P, rings_of[s["kind"]][which], m, which + "_ready")

        def project_cross_v(s):
            i = s["tile"]
            ps_n, ps, free = r_big.take()
            pe.wait(free, m_ctx, m_wv)
            for c in range(2):
                m = pe.do(lambda e, c=c: e.matmul(ps[:, c * 512:(c + 1) * 512], ctx_t[:, i * P:(i + 1) * P],
                                                  w_in[1][0:CTX_D, 2 * INNER + c * 512:2 * INNER + (c + 1) * 512],
                                                  start=True, stop=True), "v_projected" if c else None)
            s["v_n"], s["v"], s["v_m"] = evacuate(ps_n, ps, INNER, wide_rings["v"], m, "v_ready")

        def second_keys_and_values(tiles, half, which):
            ps_n, ps, free = r_big.take()
            pe.wait(free, m_ctx, m_param)
            if which == "k":
                dst = xk_all[:, 0, half * 1024:(half + 1) * 1024]
                for c in range(2):
                    at = half * 1024 + c * 512
                    m = pe.do(lambda e, c=c, at=at: e.matmul(ps[:, c * 512:(c + 1) * 512], wx[0:CTX_D, 1, :],
                                                             ctx_t[:, at:at + 512], start=True, stop=True),
                              "second_projected" if c else None)
            else:
                dst = xv_all[:, half * 1024:(half + 1) * 1024]
                for c in range(TILES // 2):
                    at = half * 1024 + c * P
                    m = pe.do(lambda e, c=c, at=at: e.matmul(ps[:, c * D:(c + 1) * D], ctx_t[:, at:at + P],
                                                             wx[0:CTX_D, 2, :], start=True, stop=True),
                              "second_projected" if c == TILES // 2 - 1 else None)
            act.wait(m)
            m = act.do(lambda e: e.activation(dst, ps[:, :], ACT.Copy), "second_" + which)
            r_big.done(ps_n, m)
            for s in tiles[half * TILES // 2:(half + 1) * TILES // 2]:
                i = s["tile"]
                s[which] = xk_all[:, :, i * P:(i + 1) * P] if which == "k" else xv_all[:, i * D:(i + 1) * D]
                s[which + "_m"] = m

        def project_layer(s, which):
            b, col = s["layer"] % 2, {"q": 0, "k": 1, "v": 2}[which]
            ps_n, ps, free = r_big.take()
            pe.wait(free, s["xt_m"], layer_loaded[s["layer"]])
            for c in range(2):
                at = col * INNER + c * 512
                m = pe.do(lambda e, c=c, at=at: e.matmul(ps[:, c * 512:(c + 1) * 512], s["xt"][:, :],
                                                         w_in[b][:, at:at + 512], start=True, stop=True),
                          "rows_projected" if c else None)
            if which == "v":
                r_xt.done(s["xt_n"], m)
                s["v_n"], s["v"], s["v_m"] = evacuate(ps_n, ps, INNER, wide_rings["v"], m, "v_ready")
                return
            s[which + "_raw"] = evacuate(ps_n, ps, INNER, r_raw, m, "rows_raw")

        def rotate(s, which):
            col = "qk".index(which)
            raw_n, raw, raw_m = s[which + "_raw"]
            heads = lambda ap: ap.rearrange("p (h d) -> p h d", d=HEAD_D)
            halves = lambda ap: ap.rearrange("p (h s d) -> p h s d", s=2, d=HEAD_D // 2)
            table = rope[:, s["layer"], 2 * col, None, :].to_broadcast([P, HEADS, HEAD_D])
            sine = rope[:, s["layer"], 2 * col + 1, :].rearrange("p (s d) -> p s d", s=2)[:, None, :, :].to_broadcast(
                [P, HEADS, 2, HEAD_D // 2])
            c_n, cs, c_free = r_cos.take()
            s_n, sn, s_free = r_sin.take()
            dve.wait(raw_m, c_free, s_free, m_rope)
            m_cos = dve.do(lambda e: e.tensor_tensor(heads(cs[:, :]), heads(raw[:, :]), table, ALU.mult), "rotated")
            m_sin = dve.do(lambda e: e.tensor_tensor(halves(sn[:, :]), halves(raw[:, :])[:, :, ::-1, :], sine, ALU.mult),
                           "rotated")
            pool.wait(m_sin)
            m_add = pool.do(lambda e: e.tensor_tensor(cs[:, :], cs[:, :], sn[:, :], ALU.add), "rotation_added")
            r_sin.done(s_n, m_add)
            s[which + "_raw"] = (raw_n, raw, raw_m, m_sin)
            s[which + "_rows"] = [c_n, cs, m_add]

        def square(s, which):
            raw_n, raw, raw_m, m_sin = s[which + "_raw"]
            sq_n, sq, sq_free = r_sq.take()
            act.wait(raw_m, sq_free)
            m = act.do(lambda e: e.activation(sq[:, :], raw[:, :], ACT.Square), "squared")
            r_raw.done(raw_n, m_sin, m)
            s[which + "_sq"] = (sq_n, sq, m)

        def sum_squares(s, which):
            sq_n, sq, m_sq = s[which + "_sq"]
            col = "qk".index(which)
            if col == 0:
                s["norm"] = r_norm.take()
            nm, n_free = s["norm"][1:]
            dve.wait(n_free, m_sq)
            s["norm_m"] = dve.do(lambda e: e.tensor_reduce(
                nm[:, 0, col, :], sq[:, :].rearrange("p (h d) -> p h d", d=HEAD_D), AX_X, ALU.add), "norm_summed")
            r_sq.done(sq_n, s["norm_m"])

        def inverse_norms(s):
            nm, m = s["norm"][1], s["norm_m"]
            dve.wait(m)
            m = dve.do(lambda e: e.tensor_scalar(nm[:, 0, :, :], nm[:, 0, :, :], NORM_FLOOR, None, ALU.max),
                       "norm_summed")
            act.wait(m)
            m = act.do(lambda e: e.activation(nm[:, 1, :, :], nm[:, 0, :, :], ACT.Ln, scale=2.0 ** LN_SHIFT), "log")
            act.wait(m)
            s["norm_m"] = act.do(lambda e: e.activation(nm[:, 2, :, :], nm[:, 1, :, :], ACT.Exp,
                                                        bias=floor_shift[:, :], scale=-0.5), "inverse_root")

        def scale_rows(s, which):
            c_n, cs, m_add = s[which + "_rows"]
            n_n, nm, _ = s["norm"]
            col = "qk".index(which)
            heads = lambda ap: ap.rearrange("p (h d) -> p h d", d=HEAD_D)
            pool.wait(m_add, s["norm_m"])
            m = pool.do(lambda e: e.tensor_tensor(
                heads(cs[:, :]), heads(cs[:, :]),
                nm[:, 2, col, :, None].to_broadcast([P, HEADS, HEAD_D]), ALU.mult), "rows_ready")
            if col == 1:
                r_norm.done(n_n, m)
            s[which + "_rows"][2] = m

        def turn(s, which):
            c_n, cs, m_rows = s[which + "_rows"]
            ps_n, ps, free = r_big.take()
            pe.wait(free, m_rows)
            for j in range(PAIRS):
                m = pe.do(lambda e, j=j: e.transpose(ps[:, j * P:(j + 1) * P], cs[:, j * P:(j + 1) * P], ident),
                          "rows_turned" if j == PAIRS - 1 else None)
            r_cos.done(c_n, m)
            s[which + "_n"], s[which], s[which + "_m"] = evacuate(
                ps_n, ps, INNER, wide_rings[which], m, which + "_ready")

        def scores(s):
            wide = s["kind"] != "X"
            pairs, hd = (PAIRS, HEAD_D) if wide else (XHEADS // 2, XHEAD_D)
            width, groups = pairs * P, pairs * 2
            masked = s["kind"] == "L"
            rings = rings_of[s["kind"]]
            step = P if wide else 512
            ps_n, ps, free = r_big.take()
            pe.wait(free, s["q_m"], s["k_m"])
            qt, kt = s["q"], s["k"]
            for n in range(pairs):
                for b in range(2):
                    for h in range(2):
                        j = (n + h * (pairs // 2)) % pairs if wide else n
                        if wide:
                            lo, jj = h * hd, j
                        else:
                            lo, jj = (2 * j + h) * hd, 0
                        last = n == pairs - 1 and b == 1 and h == 1
                        m = pe.do(lambda e, j=j, b=b, h=h, lo=lo, jj=jj: e.matmul(
                            ps[h * 64:h * 64 + 64, j * step + b * SEQ:j * step + (b + 1) * SEQ],
                            qt[lo:lo + hd, jj, b * SEQ:(b + 1) * SEQ], kt[lo:lo + hd, jj, b * SEQ:(b + 1) * SEQ],
                            start=True, stop=True), "scored" if last else None)
            rings["q"].done(s["q_n"], m)
            if wide:
                rings["k"].done(s["k_n"], m)
            scale = {"A": HEAD_D ** -0.5, "X": XHEAD_D ** -0.5, "L": 8.0}[s["kind"]]
            grouped = lambda ap: ap[:, 0:width].rearrange("p (g k) -> p g k", k=SEQ)
            p_n, p, p_free = rings["p"].take()
            t_n, sm, t_free = r_soft.take()
            score = ps[:, :].rearrange("p (j c) -> p j c", c=step)[:, 0:pairs, 0:P].rearrange(
                "p j (b k) -> p j b k", k=SEQ)
            by_pair = lambda ap: ap.rearrange("p (j b) -> p j b", b=2)
            dve.wait(m, t_free, p_free)
            if masked:
                out = p[:, 0:width].rearrange("p (j b k) -> p j b k", b=2, k=SEQ)
                m = dve.do(lambda e, score=score: e.tensor_tensor(
                    out, score, const[:, None, None, C_MASK:C_MASK + SEQ].to_broadcast([P, pairs, 2, SEQ]), ALU.add),
                    "masked")
                r_big.done(ps_n, m)
                score = out
                dve.wait(m)
            m = dve.do(lambda e: e.tensor_reduce(by_pair(sm[:, 0:groups]), score, AX_X, ALU.max), "row_max")
            dve.wait(m)
            m = dve.do(lambda e: e.tensor_tensor(
                p[:, 0:width].rearrange("p (j b k) -> p j b k", b=2, k=SEQ), score,
                by_pair(sm[:, 0:groups])[:, :, :, None].to_broadcast([P, pairs, 2, SEQ]), ALU.subtract),
                "max_subtracted")
            if not masked:
                r_big.done(ps_n, m)
            s["soft"] = (p_n, p, t_n, sm, m, width, groups, scale)

        def exponentials(s):
            p_n, p, t_n, sm, m, width, groups, scale = s["soft"]
            act.wait(m)
            s["exp_m"] = act.do(lambda e: e.activation(p[:, 0:width], p[:, 0:width], ACT.Exp, scale=scale),
                                "exponentials")

        def normalize(s):
            p_n, p, t_n, sm, m, width, groups, _ = s["soft"]
            grouped = lambda ap: ap[:, 0:width].rearrange("p (g k) -> p g k", k=SEQ)
            dve.wait(s["exp_m"])
            m = dve.do(lambda e: e.tensor_reduce(sm[:, HEADS:HEADS + groups], grouped(p), AX_X, ALU.add), "row_sum")
            dve.wait(m)
            m = dve.do(lambda e: e.reciprocal(sm[:, 2 * HEADS:2 * HEADS + groups], sm[:, HEADS:HEADS + groups]),
                       "row_sum")
            pool.wait(m)
            m = pool.do(lambda e: e.tensor_tensor(
                grouped(p), grouped(p), sm[:, 2 * HEADS:2 * HEADS + groups, None].to_broadcast([P, groups, SEQ]),
                ALU.mult), "probabilities")
            r_soft.done(t_n, m)
            s["p_m"] = m

        def turn_probabilities(s):
            p_n, p, width = s["soft"][0], s["soft"][1], s["soft"][5]
            rings = rings_of[s["kind"]]
            ps_n, ps, free = r_big.take()
            pe.wait(free, s["p_m"])
            for j in range(width // P):
                m = pe.do(lambda e, j=j: e.transpose(ps[:, j * P:(j + 1) * P], p[:, j * P:(j + 1) * P], ident),
                          "probabilities_turned" if j == width // P - 1 else None)
            rings["p"].done(p_n, m)
            s["pt_n"], s["pt"], s["pt_m"] = evacuate(ps_n, ps, width, rings["pt"], m, "pt_ready")

        def weigh(s):
            wide = s["kind"] != "X"
            pairs, hd = (PAIRS, HEAD_D) if wide else (XHEADS // 2, XHEAD_D)
            pt, v = s["pt"], s["v"]
            ps_n, ps, free = r_big.take()
            pe.wait(free, s["pt_m"], s["v_m"])
            for n in range(pairs):
                for h in range(2):
                    for b in range(2):
                        j = n
                        head = 2 * j + h
                        lo, at = (h * hd, b * 512 + j * SEQ) if wide else (head * hd, b * 512)
                        last = n == pairs - 1 and h == 1 and b == 1
                        m = pe.do(lambda e, j=j, b=b, h=h, head=head, lo=lo, at=at: e.matmul(
                            ps[lo:lo + hd, at:at + SEQ],
                            v[b * SEQ:(b + 1) * SEQ, head * hd:(head + 1) * hd],
                            pt[b * SEQ:(b + 1) * SEQ, j * P + h * SEQ:j * P + (h + 1) * SEQ],
                            start=True, stop=True), "weighed" if last else None)
            rings = rings_of[s["kind"]]
            rings["pt"].done(s["pt_n"], m)
            if wide:
                rings["v"].done(s["v_n"], m)
            n_out = PAIRS if wide else 1
            s["o_n"], o, free = rings["ot"].take()
            s["o"] = o
            act.wait(m, free)
            s["o_m"] = act.do(lambda e: e.activation(
                o[:, 0:n_out, :].rearrange("p j (b q) -> p b j q", q=SEQ), ps[:, :].rearrange("p (b j q) -> p b j q", b=2, q=SEQ)[:, :, 0:n_out, :], ACT.Copy),
                "heads_ready")
            r_big.done(ps_n, s["o_m"])

        def output(s):
            i, kind = s["tile"], s["kind"]
            o = s["o"]
            ps_n, ps, free = r_small.take()
            pe.wait(free, s["o_m"], m_const, m_param, m_wo)
            if kind != "L":
                at = R_BO0 if kind == "A" else R_BO1
                pe.do(lambda e: e.matmul(ps[:, 0:D], ones_row, rows[:, at:at + D], start=True, stop=False))
            n_in = 1 if kind == "X" else PAIRS
            for j in range(n_in):
                w = {"A": lambda j: w_out[1][:, j, :], "X": lambda j: wx[:, 3, :],
                     "L": lambda j: w_out[s["layer"] % 2][:, j, :]}[kind](j)
                m = pe.do(lambda e, j=j, w=w: e.matmul(ps[:, 0:D], o[:, j, :], w, start=(j == 0 and kind == "L"),
                                                       stop=(j == n_in - 1)), "output_projected" if j == n_in - 1 else None)
            rings_of[kind]["ot"].done(s["o_n"], m)
            dve.wait(m, x_read[i], x_ready[i])
            x_ready[i] = dve.do(lambda e: e.tensor_tensor(x[:, i, :], x[:, i, :], ps[:, 0:D], ALU.add), "x_updated")
            r_small.done(ps_n, x_ready[i])
            if kind == "X":
                dve.wait(x_ready[i])
                s["kept"] = dve.do(lambda e: e.tensor_copy(x_in[:, i, :], x[:, i, :]), "x_kept")
                s["factors"] = norm_factors(x[:, i, :], x_ready[i])
            s["done"] = m

        def enter_layers(s):
            i = s["tile"]
            dve.wait(s["kept"])
            x_ready[i] = layer_norm(x[:, i, :], s["factors"], place=x[:, i, :])[2]

        def ff_input(s):
            i = s["tile"]
            ps_n, ps, free = r_small.take()
            pe.wait(x_ready[i], free)
            m = pe.do(lambda e: e.matmul(ps[:, 0:64], shift, x[:, i, 64:128], start=True, stop=True), "shifted")
            x_read[i] = [m]
            n, xs, xs_free = r_xs.take()
            dve.wait(m, xs_free)
            m1 = dve.do(lambda e: e.tensor_copy(xs[:, 64:128], ps[:, 0:64]), "shifted_rows")
            m2 = dve.do(lambda e: e.tensor_copy(xs[:, 0:64], x[:, i, 0:64]), "shifted_rows")
            r_small.done(ps_n, m1)
            pool.wait(m2, x_read[i], m_param)
            s["biased"] = pool.do(lambda e: e.tensor_tensor(
                x[:, i, :], x[:, i, :], ff_bias[:, s["layer"], :], ALU.add), "bias_added")
            s["xs"] = (n, xs, norm_factors(xs[:, :], m2))

        def ff_norm(s):
            n, xs, factors = s["xs"]
            xn_n, xn, m = layer_norm(xs[:, :], factors)
            r_xs.done(n, m)
            s["xn"] = (xn_n, xn, m)

        def ff_turn(s):
            xn_n, xn, m = s["xn"]
            layer, g, k = s["layer"], s["group"], s["tile"] % GROUP
            ps_n, ps, free = r_small.take()
            pe.wait(m, free)
            m = pe.do(lambda e: e.transpose(ps[:, 0:P], xn[:, :], ident), "tile_turned")
            r_xn.done(xn_n, m)
            if k == 0:
                g["fx_n"], g["fx"], g["fx_free"] = r_ffx.take()
            act.wait(m, g["fx_free"], m_param)
            fx = g["fx"]
            g["fx_m"] = act.do(lambda e: e.activation(
                fx[:, k * P:(k + 1) * P], ps[:, 0:P], ACT.Identity, bias=cols[:, B_LNB + layer:B_LNB + layer + 1],
                scale=cols[:, B_LNG + layer:B_LNG + layer + 1]), "tile_copied")
            r_small.done(ps_n, g["fx_m"])

        def ff_hidden(s):
            if s["tile"] % GROUP != GROUP - 1:
                return
            layer, g = s["layer"], s["group"]
            b = layer % 2
            g["h_n"], hid, h_free = r_hid.take()
            g["h"] = hid
            for c in range(FF_CHUNKS):
                ps_n, ps, free = r_big.take()
                pe.wait(free, g["fx_m"], layer_loaded[layer])
                pe.do(lambda e, c=c, ps=ps: e.matmul(ps[:, 0:512], w_ff1[b][:, FF_CHUNKS + c, :], g["fx"][:, :],
                                                     start=True, stop=True))
                m = pe.do(lambda e, c=c, ps=ps: e.matmul(ps[:, 512:1024], w_ff1[b][:, c, :], g["fx"][:, :],
                                                         start=True, stop=True), "hidden_projected")
                at = B_FF1 + 2 * FF_CHUNKS * layer + c
                g_n, gate, g_free = r_gate.take()
                act.wait(m, g_free)
                m_g = act.do(lambda e, ps=ps, at=at, gate=gate: e.activation(
                    gate[:, :], ps[:, 0:512], ACT.Gelu,
                    bias=cols[:, at + FF_CHUNKS:at + FF_CHUNKS + 1]), "gated")
                dve.wait(m_g, h_free)
                g["h_m"] = dve.do(lambda e, ps=ps, at=at, gate=gate, c=c: e.scalar_tensor_tensor(
                    out=hid[:, c, :], in0=ps[:, 512:1024], scalar=cols[:, at:at + 1], in1=gate[:, :],
                    op0=ALU.add, op1=ALU.mult), "hidden_ready")
                r_gate.done(g_n, g["h_m"])
                r_big.done(ps_n, g["h_m"])
            exp_tables()
            r_ffx.done(g["fx_n"], m)

        def ff_output(s):
            layer, i, g = s["layer"], s["tile"], s["group"]
            k, hid = i % GROUP, g["h"]
            ps_n, ps, free = r_small.take()
            pe.wait(free, g["h_m"])
            for c in range(FF_CHUNKS):
                m = pe.do(lambda e, c=c: e.matmul(ps[:, 0:D], hid[:, c, k * P:(k + 1) * P], w_ff2[layer % 2][:, c, :],
                                                  start=(c == 0), stop=(c == FF_CHUNKS - 1)),
                          "ff_projected" if c == FF_CHUNKS - 1 else None)
            dve.wait(m, s["biased"])
            x_ready[i] = dve.do(lambda e: e.tensor_tensor(x[:, i, :], x[:, i, :], ps[:, 0:D], ALU.add), "x_updated")
            r_small.done(ps_n, x_ready[i])
            if k == GROUP - 1:
                r_hid.done(g["h_n"], m)
            if i == TILES - 1 and layer + 2 < DEPTH:
                layer_free[layer % 2] = [m]
                load_layer(layer + 2)
            if layer == DEPTH - 1:
                pool.wait(x_ready[i])
                m = pool.do(lambda e: e.tensor_tensor(x_in[:, i, :], x_in[:, i, :], x[:, i, :], ALU.add),
                            "result_ready")
                sp.wait(m)
                s["stored"] = sp.do(lambda e: e.dma_start(out[i * P:(i + 1) * P, :], x_in[:, i, :]), "stored", 16)

        r_xs = ring("xs", 2, [P, D])

        logits = sb("logits", [P, TILES, EXPERTS])
        work = ring("route_work", 2, [P, EXPERTS])
        onehot_b = sb("onehot_b", [P, TILES, EXPERTS], BF16)
        chosen_b = sb("chosen_b", [P, TILES, EXPERTS], BF16)
        top = sb("top", [P, 8, TILES])
        slot = sb("slot", [P, 2, TILES], I32)
        ffx_n, ffx_buf, _ = r_ffx.take()
        r_b2 = Ring([ffx_buf[0:1, n * D:(n + 1) * D] for n in range(4)])
        zeros_n, zeros_buf, _ = r_hid.take()
        zeros = zeros_buf[:, 0:2, :].rearrange("p a b -> p (a b)")
        dispatched = t["dispatched"]
        answers = t["answers"]

        m_z = pool.do(lambda e: e.memset(zeros, 0.0), "zeros")
        sp.wait(m_z)
        d_v = dispatched.rearrange("(h p s) d -> h p (s d)", h=2, p=P)
        for h in range(2):
            m_clear = sp.do(lambda e, h=h: e.dma_start(d_v[h], zeros), "dispatch_cleared", 16)
        m_zero_row = sp.do(lambda e: e.dma_start(answers[SLOTS:SLOTS + 1, :], zeros_buf[0:1, 0, 0:D]), "zero_row", 16)
        r_hid.done(zeros_n, m_clear, m_zero_row)

        expert_w = {}

        def load_expert(e_id):
            n1, both, free1 = r_cos.take()
            n2, b2, free2 = r_b2.take()
            w1, w2 = both[:, 0:HIDDEN], both[:, HIDDEN:].rearrange("p (c d) -> p c d", d=D)
            sp.wait(free1, free2)
            sem = f"expert_weights{n1}"
            sp.do(lambda e: e.dma_start(w1, t["mw1"][e_id]), sem, 16)
            sp.do(lambda e: e.dma_start(b2[:, :], t["mb2"][e_id:e_id + 1, :]), sem, 16)
            m = sp.do(lambda e: e.dma_start(w2, t["mw2"][e_id].rearrange("(c p) d -> p c d", p=P)), sem, 16)
            expert_w[e_id] = (n1, w1, w2, n2, b2, m)

        for e_id in range(4):
            load_expert(e_id)

        def route_factors(s):
            i = s["tile"]
            s["factors"] = norm_factors(x[:, i, :], x_ready[i])

        def route_turn(s):
            i = s["tile"]
            s["kept"] = layer_norm(x[:, i, :], s["factors"], place=x_in[:, i, :])[2]
            s["rt_n"], s["rt"], s["rt_m"], _ = transposed(x_in[:, i, :], s["kept"])

        def route_logits(s):
            i = s["tile"]
            ps_n, ps, free = r_small.take()
            pe.wait(s["rt_m"], free, m_param)
            pe.do(lambda e: e.matmul(ps[:, 0:EXPERTS], s["rt"][:, :], wg[:, :], start=True, stop=False))
            m = pe.do(lambda e: e.matmul(ps[:, 0:EXPERTS], ones_row, rows[:, R_BG:R_BG + EXPERTS],
                                         start=False, stop=True), "logits_ready")
            r_xt.done(s["rt_n"], m)
            dve.wait(m)
            s["logits"] = dve.do(lambda e: e.tensor_copy(logits[:, i, :], ps[:, 0:EXPERTS]), "logits_copied")
            r_small.done(ps_n, s["logits"])

        def chain(fn, *marks):
            dve.wait(*marks)
            m = dve.do(fn, "routing")
            dve.wait(m)
            return m

        def route_choice(s):
            i = s["tile"]
            expert = const[:, C_EXPERT:C_EXPERT + EXPERTS]
            w_n, w, w_free = work.take()
            chain(lambda e: e.tensor_reduce(top[:, 0, i:i + 1], logits[:, i, :], AX_X, ALU.max), s["logits"], w_free)
            chain(lambda e: e.tensor_scalar(w[:, :], logits[:, i, :], top[:, 0, i:i + 1], -64.0, ALU.is_ge, ALU.mult))
            chain(lambda e: e.tensor_tensor(w[:, :], w[:, :], expert, ALU.add))
            chain(lambda e: e.tensor_reduce(top[:, 3, i:i + 1], w[:, :], AX_X, ALU.min))
            chain(lambda e: e.tensor_scalar(top[:, 3, i:i + 1], top[:, 3, i:i + 1], 64.0, None, ALU.add))
            m = chain(lambda e: e.tensor_scalar(onehot_b[:, i, :], expert, top[:, 3, i:i + 1], None, ALU.is_equal))
            s["choice"] = m
            if i + 1 < TILES:
                m = chain(lambda e: e.tensor_tensor(chosen_b[:, i + 1, :], chosen_b[:, i, :], onehot_b[:, i, :],
                                                    ALU.add))
            work.done(w_n, m)

        def route_count(s):
            i = s["tile"]
            s["count_n"], ps, free = r_small.take()
            s["count"] = ps
            pe.wait(s["choice"], free, m_bf)
            pe.do(lambda e: e.matmul(ps[:, 0:EXPERTS], tri_b[:, :], onehot_b[:, i, :], start=True, stop=False))
            s["count_m"] = pe.do(lambda e: e.matmul(ps[:, 0:EXPERTS], ones_b[:, :], chosen_b[:, i, :],
                                                    start=False, stop=True), "earlier_counted")

        def route_slot(s):
            i = s["tile"]
            ps = s["count"]
            w_n, w, w_free = work.take()
            m = chain(lambda e: e.tensor_tensor(w[:, :], ps[:, 0:EXPERTS], onehot_b[:, i, :], ALU.mult),
                      s["count_m"], w_free)
            r_small.done(s["count_n"], m)
            m = chain(lambda e: e.tensor_reduce(top[:, 4, i:i + 1], w[:, :], AX_X, ALU.add))
            work.done(w_n, m)
            chain(lambda e: e.tensor_scalar(top[:, 5, i:i + 1], top[:, 3, i:i + 1], float(CAP),
                                            top[:, 4, i:i + 1], ALU.mult, ALU.add))
            chain(lambda e: e.tensor_scalar(top[:, 6, i:i + 1], top[:, 4, i:i + 1], float(CAP), float(2 * SLOTS),
                                            ALU.is_ge, ALU.mult))
            chain(lambda e: e.tensor_tensor(top[:, 5, i:i + 1], top[:, 5, i:i + 1], top[:, 6, i:i + 1], ALU.add))
            m = chain(lambda e: e.tensor_copy(slot[:, 0, i:i + 1], top[:, 5, i:i + 1]))
            pool.wait(m, m_clear, s["kept"])
            s["dispatched"] = pool.do(lambda e: e.indirect_dma_start(
                out=dispatched, out_offset=bass.IndirectOffsetOnAxis(ap=slot[:, 0, i:i + 1], axis=0),
                in_=x_in[:, i, :], in_offset=None, bounds_check=SLOTS - 1, oob_is_err=False), "dispatched", 16)
            chain(lambda e: e.tensor_scalar(top[:, 7, i:i + 1], top[:, 5, i:i + 1], float(SLOTS), None, ALU.min))
            s["slot"] = chain(lambda e: e.tensor_copy(slot[:, 1, i:i + 1], top[:, 7, i:i + 1]))

        m_chosen = dve.do(lambda e: e.memset(chosen_b[:, 0, :], 0.0), "constants_set")
        dve.wait(m_chosen)

        def gates(tiles):
            whole = [P, TILES, EXPERTS]
            m = chain(lambda e: e.tensor_tensor(logits[:, :, :], logits[:, :, :],
                                                top[:, 0, :, None].to_broadcast(whole), ALU.subtract))
            act.wait(m)
            m = act.do(lambda e: e.activation(logits[:, :, :], logits[:, :, :], ACT.Exp), "gate_exponentials")
            chain(lambda e: e.tensor_reduce(top[:, 1, :], logits[:, :, :], AX_X, ALU.add), m)
            chain(lambda e: e.reciprocal(top[:, 2, :], top[:, 1, :]))

        QUARTER = EXPERTS // 4
        tokens, replies = [], []
        by_expert = lambda ap: ap.rearrange("(e p) d -> p e d", p=P)

        def load_tokens(tiles):
            sp.wait(tiles[-1]["dispatched"])
            for h in range(2):
                tokens.append(r_raw.take())
                replies.append(r_sin.take())
                for q in range(2):
                    first = (2 * h + q) * QUARTER
                    sp.wait(tokens[h][2])
                    m = sp.do(lambda e, h=h, q=q, first=first: e.dma_start(
                        tokens[h][1][:, q * QUARTER * D:(q + 1) * QUARTER * D].rearrange("p (e d) -> p e d", d=D),
                        by_expert(dispatched[first * CAP:(first + QUARTER) * CAP, :])), f"tokens_loaded{2 * h + q}", 16)
                    for s in experts[first:first + QUARTER]:
                        s["tokens_m"] = m

        def expert_turn(s):
            h, k = divmod(s["expert"], EXPERTS // 2)
            n, buf, _ = tokens[h]
            s["xt_n"], s["xt"], s["xt_m"], m = transposed(buf[:, k * D:(k + 1) * D], s["tokens_m"])
            if k == EXPERTS // 2 - 1:
                r_raw.done(n, m)

        def expert_hidden(s):
            w1, xt = expert_w[s["expert"]][1], s["xt"]
            ps_n, ps, free = r_big.take()
            pe.wait(free, s["xt_m"], expert_w[s["expert"]][5])
            for c in range(HIDDEN // P):
                m = pe.do(lambda e, c=c: e.matmul(
                    ps[:, c * P:(c + 1) * P], w1[:, c * P:(c + 1) * P], xt[:, :], start=True, stop=True),
                    "expert_hidden" if c == HIDDEN // P - 1 else None)
            r_xt.done(s["xt_n"], m)
            s["h_n"], hb, h_free = r_sq.take()
            s["h"] = hb
            act.wait(m, h_free, m_param)
            for c in range(HIDDEN // P):
                at = B_MOE1 + s["expert"] * (HIDDEN // P) + c
                m = act.do(lambda e, c=c, at=at: e.activation(
                    hb[:, c * P:(c + 1) * P], ps[:, c * P:(c + 1) * P], ACT.Relu, bias=cols[:, at:at + 1]),
                    "expert_relu")
            r_big.done(ps_n, m)
            s["h_m"] = m

        def expert_output(s):
            n1, _, w2, n2, b2, _ = expert_w[s["expert"]]
            hb = s["h"]
            ps_n, ps, free = r_small.take()
            pe.wait(free, s["h_m"])
            pe.do(lambda e: e.matmul(ps[:, 0:D], ones_row, b2[:, :], start=True, stop=False))
            for c in range(HIDDEN // P):
                m = pe.do(lambda e, c=c: e.matmul(
                    ps[:, 0:D], hb[:, c * P:(c + 1) * P], w2[:, c, :], start=False, stop=(c == HIDDEN // P - 1)),
                    "expert_output" if c == HIDDEN // P - 1 else None)
            s["output_m"] = m
            r_b2.done(n2, m)
            r_cos.done(n1, m)
            r_sq.done(s["h_n"], m)
            h, k = divmod(s["expert"], EXPERTS // 2)
            n, y, y_free = replies[h]
            dve.wait(m, y_free)
            m = dve.do(lambda e: e.tensor_copy(y[:, k * D:(k + 1) * D], ps[:, 0:D]), "answer_copied")
            r_small.done(ps_n, m)
            if k % QUARTER == QUARTER - 1:
                first, at = s["expert"] + 1 - QUARTER, (k + 1 - QUARTER) * D
                act.wait(m)
                m = act.do(lambda e: e.dma_start(
                    by_expert(answers[first * CAP:(first + QUARTER) * CAP, :]),
                    y[:, at:at + QUARTER * D].rearrange("p (e d) -> p e d", d=D)), "answers_stored", 16)
                if k == EXPERTS // 2 - 1:
                    r_sin.done(n, m)
                answered.append(m)
            if s["expert"] + 4 < EXPERTS:
                load_expert(s["expert"] + 4)

        answered = []

        def fetch_answers(tiles, takers):
            pool.wait(tiles[-1]["dispatched"], tiles[-1]["slot"], answered[-1], m_zero_row)
            for s in takers:
                i = s["tile"]
                s["back"] = pool.do(lambda e, i=i: e.indirect_dma_start(
                    out=x_in[:, i, :], out_offset=None, in_=answers,
                    in_offset=bass.IndirectOffsetOnAxis(ap=slot[:, 1, i:i + 1], axis=0),
                    bounds_check=SLOTS, oob_is_err=False), f"answer_fetched{i}", 16)

        def add_answer(s):
            i = s["tile"]
            dve.wait(s["back"])
            x_ready[i] = dve.do(lambda e: e.scalar_tensor_tensor(
                out=x[:, i, :], in0=x_in[:, i, :], scalar=top[:, 2, i:i + 1], in1=x[:, i, :],
                op0=ALU.mult, op1=ALU.add), "x_updated")

        def run(stages):
            for step in range(max(len(items) + lag for _, items, lag in stages)):
                for stage, items, lag in stages:
                    if 0 <= step - lag < len(items):
                        stage(items[step - lag])

        project = lambda which: lambda s: (project_layer if s["kind"] == "L" else project_cross)(s, which)
        turn_of = lambda which: lambda s: turn(s, which)

        first = [{"kind": "A", "tile": i} for i in range(TILES)]
        run([
            (scores, first, 2),
            (route_logits, first, 5),
            (turn_probabilities, first, 3),
            (project("k"), first, 1),
            (route_choice, first, 5),
            (exponentials, first, 2),
            (input_factors, first, 0),
            (weigh, first, 3),
            (project("q"), first, 1),
            (normalize, first, 2),
            (route_factors, first, 4),
            (project_cross_v, first, 1),
            (input_norm, first, 0),
            (input_turn, first, 0),
            (route_turn, first, 4),
            (route_count, first, 5),
            (route_slot, first, 5),
            (output, first, 3),
        ])
        layer_free[1] = [first[-1]["done"]]
        experts = [{"expert": n} for n in range(EXPERTS)]
        load_tokens(first)
        gates(first)
        second = [{"kind": "X", "tile": i} for i in range(TILES)]
        for part in range(2):
            second_keys_and_values(second, part, "k")
        run([
            (expert_turn, experts, 0),
            (expert_hidden, experts, 1),
            (expert_output, experts, 2),
        ])
        r_ffx.done(ffx_n, experts[-1]["output_m"])
        fetch_answers(first, second)
        for part in range(2):
            second_keys_and_values(second, part, "v")
        load_layer(1)

        groups = [[{} for _ in range(TILES // GROUP)] for _ in range(DEPTH)]
        layers = [{"kind": "L", "layer": n, "tile": i, "group": groups[n][i // GROUP]}
                  for n in range(DEPTH) for i in range(TILES)]
        start = 6
        of = lambda stage, which: lambda s: stage(s, which)
        run([
            (scores, layers, start + 2),
            (turn_probabilities, layers, start + 3),
            (scores, second, 3),
            (project("q"), layers, start),
            (ff_input, layers, start + 4),
            (exponentials, layers, start + 2),
            (exponentials, second, 3),
            (input_norm, second, 1),
            (add_answer, second, 0),
            (input_factors, second, 0),
            (of(rotate, "q"), layers, start),
            (turn_probabilities, second, 4),
            (project("k"), layers, start),
            (normalize, layers, start + 2),
            (normalize, second, 3),
            (of(rotate, "k"), layers, start),
            (ff_norm, layers, start + 4),
            (of(square, "q"), layers, start),
            (weigh, layers, start + 3),
            (ff_hidden, layers, start + 5),
            (weigh, second, 4),
            (project("q"), second, 2),
            (input_turn, second, 1),
            (project("v"), layers, start),
            (output, second, 4),
            (of(square, "k"), layers, start),
            (ff_output, layers, start + 8),
            (of(sum_squares, "q"), layers, start),
            (turn_of("q"), layers, start + 1),
            (turn_of("k"), layers, start + 1),
            (of(sum_squares, "k"), layers, start),
            (ff_turn, layers, start + 4),
            (inverse_norms, layers, start),
            (of(scale_rows, "q"), layers, start),
            (of(scale_rows, "k"), layers, start),
            (enter_layers, second, 4),
            (output, layers, start + 3),
            (input_layer, layers, start - 1),
        ])
        sp.wait(layers[-1]["stored"])

        sems = {name: ctx.enter_context(nc.semaphore(name)) for name in counts}
        block = ctx.enter_context(nc.Block())

        @block.sync
        def _(e):
            sp.play(e, sems)

        @block.scalar
        def _(e):
            act.play(e, sems)

        @block.gpsimd
        def _(e):
            pool.play(e, sems)

        @block.vector
        def _(e):
            dve.play(e, sems)

        @block.tensor
        def _(e):
            pe.play(e, sems)


def shape_constants():
    f = np.float32
    c = np.zeros((P, C_END), f)
    tok = np.arange(P)
    c[:, C_IDENT:C_IDENT + P] = np.eye(P)
    c[:, C_SHIFT:C_SHIFT + P] = (tok[:, None] + 1 == tok[None, :]) & (tok[None, :] % SEQ != 0)
    c[:, C_TRI:C_TRI + P] = tok[:, None] < tok[None, :]
    c[:, C_ONES:C_ONES + P] = 1.0
    q, k = (tok % SEQ)[:, None], np.arange(SEQ)[None, :]
    c[:, C_MASK:C_MASK + SEQ] = np.where((k <= q) & (q <= k + WINDOW), 0.0, MASKED)
    half = np.arange(0, HEAD_D, 2, dtype=f)
    inv_freq = (f(1.0) / (f(10000.0) ** (half / f(HEAD_D)))).astype(f)
    pos = np.arange(SEQ, dtype=f)
    freqs = (pos[:, None] * inv_freq[None, :]).astype(f)
    base = ((half + f(0.4 * HEAD_D)) / f(1.4 * HEAD_D)).astype(f)
    power = ((pos - f(SEQ // 2)) / f(WINDOW // 2)).astype(f)
    scale = (base[None, :] ** power[:, None]).astype(f)
    cos, sin = np.cos(freqs).astype(f), np.sin(freqs).astype(f)
    for s, sc in enumerate((scale, f(1.0) / scale)):
        block = np.concatenate([cos * sc, cos * sc, -sin * sc, sin * sc], 1)
        c[:, C_ROPE + 2 * s * HEAD_D:C_ROPE + 2 * (s + 1) * HEAD_D] = np.tile(block, (2, 1))
    c[:, C_EXPERT:C_EXPERT + EXPERTS] = np.arange(EXPERTS)
    return c


def kernel(**inputs):
    import concourse.bacc as bacc
    from concourse.bass_utils import run_bass_kernel_spmd

    v = {k: np.ascontiguousarray(a) for k, a in inputs.items()}
    chunks = 2 * FF_CHUNKS
    ff1 = np.zeros((DEPTH, D, 2, FF_CHUNKS * P), np.float32)
    ff1[:, :, :, :FF] = v["L1_ffn_W1"].reshape(DEPTH, D, 2, FF)
    ffb = np.zeros((DEPTH, 2, FF_CHUNKS * P), np.float32)
    ffb[:, :, :FF] = v["L1_ffn_b1"].reshape(DEPTH, 2, FF)
    ff2 = np.zeros((DEPTH, FF_CHUNKS * P, D), np.float32)
    ff2[:, :FF] = v["L1_ffn_W2"]
    cols = np.concatenate([
        v["L0_ffn_b1"].reshape(EXPERTS * HIDDEN // P, P).T,
        ffb.reshape(DEPTH * chunks, P).T, v["L1_ffn_ln_g"].T, v["L1_ffn_ln_b"].T], 1)
    rows = np.concatenate([v["L0_xattn_bo"], v["L0_ffn_bg"], v["L1_xattn_bo"]])[None]
    wx = np.zeros((P, 4, D), np.float32)
    for n, name in enumerate(("Wq", "Wk", "Wv", "Wo")):
        w = v["L1_xattn_" + name].T
        wx[:w.shape[0], n] = w
    arrays = {
        "const": shape_constants(),
        "x": v["x"].reshape(-1, D),
        "ctx_t": np.ascontiguousarray(v["ctx_768"].reshape(-1, CTX_D).T),
        "wq": v["L0_xattn_Wq"], "wk": v["L0_xattn_Wk"], "wv": v["L0_xattn_Wv"], "wo": v["L0_xattn_Wo"],
        "cols": np.ascontiguousarray(cols), "rows": np.ascontiguousarray(rows), "wx": wx,
        "wg": v["L0_ffn_Wg"],
        "scales": np.stack([v["L1_ffn_q_scale"], v["L1_ffn_k_scale"]])[None],
        "ff_bias": v["L1_ffn_b2"][None],
        "wqkv": v["L1_ffn_Wqkv"], "lwo": v["L1_ffn_Wo"],
        "ff1": ff1.reshape(DEPTH, D, chunks, P), "ff2": ff2,
        "mw1": v["L0_ffn_W1"], "mw2": v["L0_ffn_W2"], "mb2": v["L0_ffn_b2"],
    }
    nc = bacc.Bacc("TRN2", target_bir_lowering=False, num_devices=1)
    t = {name: nc.dram_tensor(name + "_dram", a.shape, mybir.dt.from_np(a.dtype), kind="ExternalInput").ap()
         for name, a in arrays.items()}
    t["dispatched"] = nc.dram_tensor("dispatched", [SLOTS, D], F32, kind="Internal").ap()
    t["answers"] = nc.dram_tensor("answers", [SLOTS + 1, D], F32, kind="Internal").ap()
    out = nc.dram_tensor("out_dram", [BATCH * SEQ, D], F32, kind="ExternalOutput").ap()
    build(nc, t, out)
    r = run_bass_kernel_spmd(nc, [{name + "_dram": a for name, a in arrays.items()}], core_ids=[0])
    return r.results[0]["out_dram"].reshape(BATCH, SEQ, D)
```
